# Optimizing a Trainium2 kernel written in Bass

```python
import numpy as np
import jax
import jax.numpy as jnp

def _softmax(x, axis=-1):
    return jax.nn.softmax(x, axis=axis)

def _gelu(x):
    return jax.nn.gelu(x, approximate=True)

def _silu(x):
    return jax.nn.silu(x)

def _sigmoid(x):
    return jax.nn.sigmoid(x)

def _layernorm(x, axis=-1, eps=1e-05):
    m = jnp.mean(x, axis=axis, keepdims=True)
    v = jnp.var(x, axis=axis, keepdims=True)
    return (x - m) / jnp.sqrt(v + eps)

def _scatter_add(tgt, idx, src, axis=0):
    return tgt.at[idx].add(src)

def _segment_sum(src, seg, n):
    return jax.ops.segment_sum(src, seg, n)
kernel_name = 'mk_decoder_postln_d1_seqx_r4_5ae26f'

def setup_inputs(seed: int=0):
    np.random.seed(seed)
    _w = jnp.asarray

    def _rec_inputs():
        import jax
        import jax.numpy as jnp
        _rk = jax.random.key(seed)
        x = -0.0002928 + 1 * jax.random.normal(jax.random.fold_in(_rk, 1), (16, 112, 256), jnp.float32)
        _lenS = 112 - jax.random.randint(jax.random.fold_in(_rk, 7), (16,), 0, max(1, 112 // 4) + 1, jnp.int32)
        _lenS2 = 375 - jax.random.randint(jax.random.fold_in(_rk, 8), (16,), 0, max(1, 375 // 4) + 1, jnp.int32)
        _ctx_768P = jax.random.normal(jax.random.fold_in(_rk, 11), (16, 16, 192), jnp.float32)
        _ctx_768c = jax.random.dirichlet(jax.random.fold_in(_rk, 511), 0.3 * jnp.ones((16,), jnp.float32), (16, 375))
        _ctx_768t = jnp.einsum('bsk,bkd->bsd', _ctx_768c, _ctx_768P)
        _ctx_768t = _ctx_768t * jax.lax.rsqrt(jnp.mean(jnp.square(_ctx_768t)) + 1e-12) * 0.953939
        ctx_768 = 2.09791e-05 + 1.00001 * (_ctx_768t + 0.3 * jax.random.normal(jax.random.fold_in(_rk, 611), (16, 375, 192), jnp.float32))
        return (x, ctx_768)
    x, ctx_768 = _rec_inputs()

    def _L0_attn_setup():
        import jax, jax.numpy as jnp
        import numpy as np
        NUM_HEADS = 16
        GROUP_SIZE = 4
        DIM = 256
        HEAD_DIM = DIM // NUM_HEADS
        NUM_GROUPS = max(1, NUM_HEADS // GROUP_SIZE)
        SCALE = HEAD_DIM ** (-0.5)
        key = jax.random.key(seed)
        k1, k2, k3, k4, k5 = jax.random.split(key, 5)
        B, T = (1, 1024)
        x = jax.random.normal(k1, (B, T, DIM), dtype=jnp.float32)
        Wq = jax.random.normal(k2, (DIM, NUM_HEADS * HEAD_DIM), dtype=jnp.float32) * DIM ** (-0.5)
        Wk = jax.random.normal(k3, (DIM, NUM_GROUPS * HEAD_DIM), dtype=jnp.float32) * DIM ** (-0.5)
        Wv = jax.random.normal(k4, (DIM, NUM_GROUPS * HEAD_DIM), dtype=jnp.float32) * DIM ** (-0.5)
        Wo = jax.random.normal(k5, (NUM_HEADS * HEAD_DIM, DIM), dtype=jnp.float32) * DIM ** (-0.5)
        return {'x': x, 'Wq': Wq, 'Wk': Wk, 'Wv': Wv, 'Wo': Wo}
    _L0_attn_all = _L0_attn_setup()
    _L0_attn_in = {k: v for k, v in _L0_attn_all.items() if k in ('Wq', 'Wk', 'Wv', 'Wo')}
    del _L0_attn_all

    def _L0_xattn_setup():
        import jax, jax.numpy as jnp
        import numpy as np
        HEADS = 8
        DIM_HEAD = 128
        ATTN_MATRIX_SCALE = 1.5
        SCALE = DIM_HEAD ** (-0.5)

        def _split_heads(t):
            b, n, _ = t.shape
            t = t.reshape(b, n, HEADS, DIM_HEAD)
            return t.transpose(2, 0, 1, 3).reshape(HEADS, b * n, DIM_HEAD)
        key = jax.random.key(seed)
        ks = jax.random.split(key, 7)
        b, n, m = (2, 512, 512)
        qd, cd, inner = (256, 192, HEADS * DIM_HEAD)
        x = jax.random.normal(ks[0], (b, n, qd), dtype=jnp.float32)
        context = jax.random.normal(ks[1], (b, m, cd), dtype=jnp.float32)
        Wq = jax.random.normal(ks[2], (qd, inner), dtype=jnp.float32) * qd ** (-0.5)
        Wk = jax.random.normal(ks[3], (cd, inner), dtype=jnp.float32) * cd ** (-0.5)
        Wv = jax.random.normal(ks[4], (cd, inner), dtype=jnp.float32) * cd ** (-0.5)
        Wout = jax.random.normal(ks[5], (inner, qd), dtype=jnp.float32) * inner ** (-0.5)
        bout = jnp.zeros((qd,), dtype=jnp.float32)
        return {'x': x, 'context': context, 'Wq': Wq, 'Wk': Wk, 'Wv': Wv, 'Wout': Wout, 'bout': bout}
    _L0_xattn_all = _L0_xattn_setup()
    _L0_xattn_in = {k: v for k, v in _L0_xattn_all.items() if k in ('Wq', 'Wk', 'Wv', 'Wout', 'bout')}
    del _L0_xattn_all

    def _L0_ffn_setup():
        import jax, jax.numpy as jnp
        import numpy as np
        EMB = 256
        FF = 4 * EMB

        def _ternary(w):
            scale = jnp.maximum(jnp.mean(jnp.abs(w)), 1e-08)
            w_t = jnp.clip(jnp.round(w / scale), -1.0, 1.0)
            return w + jax.lax.stop_gradient(w_t - w)
        key = jax.random.key(seed)
        kx, k1, k2, kb1, kb2 = jax.random.split(key, 5)
        x = jax.random.normal(kx, (4, 512, EMB), dtype=jnp.float32)
        lim1 = 1.0 / np.sqrt(EMB)
        lim2 = 1.0 / np.sqrt(FF)
        W1 = jax.random.uniform(k1, (FF, EMB), jnp.float32, -lim1, lim1)
        b1 = jax.random.uniform(kb1, (FF,), jnp.float32, -lim1, lim1)
        W2 = jax.random.uniform(k2, (EMB, FF), jnp.float32, -lim2, lim2)
        b2 = jax.random.uniform(kb2, (EMB,), jnp.float32, -lim2, lim2)
        return {'x': x, 'W1': W1, 'b1': b1, 'W2': W2, 'b2': b2}
    _L0_ffn_all = _L0_ffn_setup()
    _L0_ffn_in = {k: v for k, v in _L0_ffn_all.items() if k in ('W1', 'b1', 'W2', 'b2')}
    del _L0_ffn_all
    return {'x': x, 'ctx_768': ctx_768, 'L0_attn_Wq': _L0_attn_in['Wq'], 'L0_attn_Wk': _L0_attn_in['Wk'], 'L0_attn_Wv': _L0_attn_in['Wv'], 'L0_attn_Wo': _L0_attn_in['Wo'], 'L0_xattn_Wq': _L0_xattn_in['Wq'], 'L0_xattn_Wk': _L0_xattn_in['Wk'], 'L0_xattn_Wv': _L0_xattn_in['Wv'], 'L0_xattn_Wout': _L0_xattn_in['Wout'], 'L0_xattn_bout': _L0_xattn_in['bout'], 'L0_ffn_W1': _L0_ffn_in['W1'], 'L0_ffn_b1': _L0_ffn_in['b1'], 'L0_ffn_W2': _L0_ffn_in['W2'], 'L0_ffn_b2': _L0_ffn_in['b2']}

def reference(x, ctx_768, L0_attn_Wq, L0_attn_Wk, L0_attn_Wv, L0_attn_Wo, L0_xattn_Wq, L0_xattn_Wk, L0_xattn_Wv, L0_xattn_Wout, L0_xattn_bout, L0_ffn_W1, L0_ffn_b1, L0_ffn_W2, L0_ffn_b2):
    import jax
    import jax.numpy as jnp

    def _L0_attn_ref(x, Wq, Wk, Wv, Wo):
        import jax, jax.numpy as jnp
        import numpy as np
        NUM_HEADS = 16
        GROUP_SIZE = 4
        DIM = 256
        HEAD_DIM = DIM // NUM_HEADS
        NUM_GROUPS = max(1, NUM_HEADS // GROUP_SIZE)
        SCALE = HEAD_DIM ** (-0.5)
        B, T, C = x.shape
        rep = NUM_HEADS // NUM_GROUPS
        q = (x @ Wq).reshape(B, T, NUM_HEADS, HEAD_DIM)
        k = (x @ Wk).reshape(B, T, NUM_GROUPS, HEAD_DIM)
        v = (x @ Wv).reshape(B, T, NUM_GROUPS, HEAD_DIM)
        k = jnp.repeat(k, rep, axis=2)
        v = jnp.repeat(v, rep, axis=2)
        scores = jnp.einsum('bqhd,bkhd->bhqk', q, k) * SCALE
        weights = jax.nn.softmax(scores, axis=-1)
        out = jnp.einsum('bhqk,bkhd->bqhd', weights, v)
        out = out.reshape(B, T, NUM_HEADS * HEAD_DIM)
        return out @ Wo

    def _L0_xattn_ref(x, context, Wq, Wk, Wv, Wout, bout):
        import jax, jax.numpy as jnp
        import numpy as np
        HEADS = 8
        DIM_HEAD = 128
        ATTN_MATRIX_SCALE = 1.5
        SCALE = DIM_HEAD ** (-0.5)

        def _split_heads(t):
            b, n, _ = t.shape
            t = t.reshape(b, n, HEADS, DIM_HEAD)
            return t.transpose(2, 0, 1, 3).reshape(HEADS, b * n, DIM_HEAD)
        b, n, _ = x.shape
        qh = _split_heads(jnp.einsum('bnq,qi->bni', x, Wq))
        kh = _split_heads(jnp.einsum('bmc,ci->bmi', context, Wk))
        vh = _split_heads(jnp.einsum('bmc,ci->bmi', context, Wv))
        sim = jnp.einsum('hid,hjd->hij', qh, kh) * SCALE
        mean = jnp.mean(sim, axis=-1, keepdims=True)
        sim = (sim - mean) * ATTN_MATRIX_SCALE + mean
        attn = jax.nn.softmax(sim, axis=-1)
        out = jnp.einsum('hij,hjd->hid', attn, vh)
        out = out.reshape(HEADS, b, n, DIM_HEAD).transpose(1, 2, 0, 3)
        out = out.reshape(b, n, HEADS * DIM_HEAD)
        return jnp.einsum('bni,iq->bnq', out, Wout) + bout

    def _L0_ffn_ref(x, W1, b1, W2, b2):
        import jax, jax.numpy as jnp
        import numpy as np
        EMB = 256
        FF = 4 * EMB

        def _ternary(w):
            scale = jnp.maximum(jnp.mean(jnp.abs(w)), 1e-08)
            w_t = jnp.clip(jnp.round(w / scale), -1.0, 1.0)
            return w + jax.lax.stop_gradient(w_t - w)
        h = jnp.einsum('bsd,fd->bsf', x, _ternary(W1)) + b1
        h = jax.nn.gelu(h, approximate=False)
        out = jnp.einsum('bsf,df->bsd', h, _ternary(W2)) + b2
        return out
    x = _layernorm(x + _L0_attn_ref(x, L0_attn_Wq, L0_attn_Wk, L0_attn_Wv, L0_attn_Wo), axis=-1)
    x = _layernorm(x + _L0_xattn_ref(x, ctx_768, L0_xattn_Wq, L0_xattn_Wk, L0_xattn_Wv, L0_xattn_Wout, L0_xattn_bout), axis=-1)
    x = _layernorm(x + _L0_ffn_ref(x, L0_ffn_W1, L0_ffn_b1, L0_ffn_W2, L0_ffn_b2), axis=-1)
    return x

_drawn_inputs = setup_inputs


def setup_inputs(seed=0):
    import zlib

    import numpy as np

    out = dict(_drawn_inputs(seed))
    spreads = {'L0_xattn_bout': (0.0, 0.1)}
    factors = {'L0_ffn_b1': 24.129, 'L0_ffn_b2': 64.0}
    for name, (base, spread) in spreads.items():
        noise = np.random.default_rng([zlib.crc32(name.encode()), seed]).standard_normal(out[name].shape)
        drawn = base * np.exp(spread * noise) if base else spread * noise
        out[name] = jnp.asarray(drawn.astype(out[name].dtype))
    for name, factor in factors.items():
        out[name] = (out[name] * factor).astype(out[name].dtype)
    return out
```

```python
from contextlib import ExitStack

import concourse.bass as bass
from concourse import mybir

F32 = mybir.dt.float32
F16 = mybir.dt.float16
ALU = mybir.AluOpType
ACT = mybir.ActivationFunctionType
AX = mybir.AxisListType

P = 128
NB, T, D = 16, 112, 256
NT = NB * T
NH_S, NG, DH_S = 16, 4, 16
NJ = NH_S // NG
DPAD = 32
SC, CD = 375, 192
NKEY = NB * SC
NH, DH = 8, 128
INNER = NH * DH
FF = 4 * D
LN_EPS = 1e-5
WSCALE = 32.0

KT = 125
NKT = NKEY // KT
GT = 4
NGRP = NKT // GT
QB = 256
NQB = NT // QB
QT = QB // P
KC = 500
NKC = NKEY // KC
QC = 448
NQC = NT // QC
VW = 2 * DH + 1
KPAD = 16
SIM_SCALE = 1.5 * DH ** -0.5
LIFT = 5.545177444479562 / SIM_SCALE

WA_Q, WA_K, WA_V = 0, NJ * P, NJ * P + P
WA_N = WA_V + NG * DH_S

CH = 1000



def build(nc, xT, x, WA, Wo, ctxT, Wq, Wk, Wv, Wout, bout, W1T, b1, W2T, b2, o_dram, out):
    with ExitStack() as top:
        def sb(stack, name, shape, dt):
            return stack.enter_context(nc.sbuf_tensor(name, shape, dt))

        def sem(name):
            return top.enter_context(nc.semaphore(name))

        def credit(eng, s, n):
            eng.sem_inc(s, n)

        psum = top.enter_context(nc.psum_tensor("psum", [P, 8, 512], F32))

        res = sb(top, "res", [T, NB, D], F32)
        yT_hi = sb(top, "yT_hi", [P, 2, NT], F16)
        yT_lo = sb(top, "yT_lo", [P, 2, NT], F16)
        ident = sb(top, "ident", [P, P], F32)
        ones = sb(top, "ones", [P, P], F32)
        wout_hi = sb(top, "wout_hi", [P, NH, D], F16)
        wout_lo = sb(top, "wout_lo", [P, NH, D], F16)
        stats = sb(top, "stats", [T, NB, 6], F32)
        meanvar = sb(top, "meanvar", [T, NB, 2], F32)
        rstd = sb(top, "rstd", [T, NB], F32)
        norm_buf = [sb(top, f"norm_buf{r}", [T, D], F32) for r in range(2)]

        def counted(eng, start, end, step):
            return eng.Fori(start, end - step + 1, step)

        def chain(eng, s):
            n = [0]

            def run(ins):
                n[0] += 1
                ins.then_inc(s, 1)
                eng.wait_ge(s, n[0])
            return run

        def layer_norm(tag, to_dram=False):
            s_agg, s_sq, s_r = sem(tag + "agg"), sem(tag + "sqrt"), sem(tag + "rstd")
            s_n, s_t, s_hi, s_lo, s_cp = [sem(tag + n) for n in ("norm", "tr", "hi", "lo", "copy")]
            s_st = [sem(f"{tag}store{r}") for r in range(2)]
            with nc.Block() as block:

                @block.vector
                def _(v):
                    credit(v, s_lo, 2)
                    for b in range(NB):
                        v.bn_aggr(meanvar[:, b, :], stats[:, b, :]).then_inc(s_agg, 1)
                    v.wait_ge(s_agg, NB)
                    v.tensor_scalar(rstd[:, :], meanvar[:, :, 1], LN_EPS, None, ALU.add).then_inc(s_agg, 1)
                    v.wait_ge(s_sq, 1)
                    v.reciprocal(rstd[:, :], rstd[:, :]).then_inc(s_r, 1)
                    v.wait_ge(s_r, 1)
                    with counted(v, 0, NB, 2) as b:
                        for r in range(2):
                            if to_dram:
                                v.wait_ge(s_st[r], b * 8 + 16)
                            else:
                                v.wait_ge(s_cp, b + r + 1)
                                v.wait_ge(s_t, b + r + 1)
                            v.tensor_scalar(norm_buf[r][:, :], res[:, b + r, :], meanvar[:, b + r, 0:1],
                                            rstd[:, bass.ds(b + r, 1)], ALU.subtract, ALU.mult).then_inc(s_n, 1)
                            if not to_dram:
                                v.wait_ge(s_hi, b + r + 1)
                                v.tensor_tensor(yT_lo[:, :, bass.ds((b + r) * T, T)],
                                                psum[:, r, 0:2 * T].rearrange("p (k t) -> p k t", k=2),
                                                yT_hi[:, :, bass.ds((b + r) * T, T)],
                                                ALU.subtract).then_inc(s_lo, 1)

                @block.scalar
                def _(a):
                    a.wait_ge(s_agg, NB + 1)
                    a.activation(rstd[:, :], rstd[:, :], ACT.Sqrt).then_inc(s_sq, 1)
                    if not to_dram:
                        with counted(a, 0, NB, 2) as b:
                            for r in range(2):
                                a.wait_ge(s_t, b + r + 3)
                                a.activation(yT_hi[:, :, bass.ds((b + r) * T, T)],
                                             psum[:, r, 0:2 * T].rearrange("p (k t) -> p k t", k=2),
                                             ACT.Copy).then_inc(s_hi, 1)

                @block.gpsimd
                def _(g):
                    if to_dram:
                        return
                    credit(g, s_cp, 2)
                    with counted(g, 0, NB, 2) as b:
                        for r in range(2):
                            g.wait_ge(s_n, b + r + 1)
                            g.tensor_copy(res[:, b + r, :], norm_buf[r][:, :]).then_inc(s_cp, 1)

                @block.tensor
                def _(pe):
                    if to_dram:
                        return
                    credit(pe, s_t, 2)
                    with counted(pe, 0, NB, 2) as b:
                        for r in range(2):
                            pe.wait_ge(s_n, b + r + 1)
                            pe.wait_ge(s_lo, b + r + 1)
                            for k in range(2):
                                mm = pe.transpose(psum[:, r, k * T:(k + 1) * T],
                                                  norm_buf[r][:, k * P:(k + 1) * P], ident[0:T, 0:T])
                            mm.then_inc(s_t, 1)

                @block.sync
                def _(sp):
                    if not to_dram:
                        return
                    for r in range(2):
                        credit(sp, s_st[r], 16)
                    with counted(sp, 0, NB, 2) as b:
                        for r in range(2):
                            sp.wait_ge(s_n, b + r + 1)
                            sp.dma_start(out[bass.ds((b + r) * T, T), :], norm_buf[r][:, :]).then_inc(
                                s_st[r], 16)
                    for r in range(2):
                        sp.wait_ge(s_st[r], 16 + NB * 8)

        with ExitStack() as ab:
            ctx_hi = sb(ab, "ctx_hi", [P, NKEY + KPAD], F16)
            ctx_lo = sb(ab, "ctx_lo", [P, NKEY + KPAD], F16)
            ctx_s = sb(ab, "ctx_s", [P, NKEY + KPAD], F16)
            wq_hi = sb(ab, "wq_hi", [P, 2, INNER], F16)
            wq_lo = sb(ab, "wq_lo", [P, 2, INNER], F16)
            wkv = {n: [sb(ab, f"w{n}_{part}", [P, INNER], F16) for part in ("hi", "lo", "s_hi", "s_lo")]
                   for n in "kv"}

            with ExitStack() as pa:
                scratch = sb(pa, "scratch", [P, 6 * 8 * T], F32)
                x32 = scratch[:, 0:2 * NT].rearrange("p (k t) -> p k t", k=2)
                wa32 = scratch[:, 2 * NT:2 * NT + 2 * WA_N].rearrange("p (k n) -> p k n", k=2)
                tiles = [scratch[0:T, i * 8 * T:(i + 1) * 8 * T].rearrange("p (h t) -> p h t", h=8)
                         for i in range(6)]
                shifted, prob, probT = tiles[0:2], tiles[2:4], tiles[4:6]
                wa_hi = sb(pa, "wa_hi", [P, 2, WA_N], F16)
                wa_lo = sb(pa, "wa_lo", [P, 2, WA_N], F16)
                wo32 = sb(pa, "wo32", [P, 2, D], F32)
                q_hi = sb(pa, "q_hi", [P, NJ, NT], F16)
                q_lo = sb(pa, "q_lo", [P, NJ, NT], F16)
                kb_hi = sb(pa, "kb_hi", [P, NG, NT], F16)
                kb_lo = sb(pa, "kb_lo", [P, NG, NT], F16)
                vs = sb(pa, "vs", [T, NB, NG, DH_S + 1], F32)
                stage = [sb(pa, f"stage{r}", [P, 2, INNER], F32) for r in range(2)]
                mx = [sb(pa, f"mx{r}", [T, 8], F32) for r in range(2)]
                rden = sb(pa, "rden", [T, 8], F32)
                att = sb(pa, "att", [T, D], F32)
                attT = sb(pa, "attT", [P, 2, T], F32)

                s_x, s_wa, s_wo, s_res = sem("a_x"), sem("a_wa"), sem("a_wo"), sem("a_res")
                s_stage = [sem(f"a_stage{r}") for r in range(2)]
                s_staged = sem("a_staged")
                s_const, s_g, s_prep, s_split = sem("a_const"), sem("a_g"), sem("a_prep"), sem("a_split")
                s_pj, s_ph, s_pl = sem("a_pj"), sem("a_ph"), sem("a_pl")
                (s_s, s_mx, s_sub, s_exp, s_T, s_ptc, s_av, s_rd, s_nrm, s_at, s_atc, s_wop, s_add, s_bn) = [
                    sem("a_" + n) for n in ("s", "mx", "sub", "exp", "T", "ptc", "av", "rd", "nrm", "at",
                                            "atc", "wop", "add", "bn")]

                def halves(n, src):
                    return [(lambda st: st[:, 0, 0:n], src[0:P]), (lambda st: st[0:64, 1, 0:n], src[P:CD]),
                            (lambda st: st[64:P, 1, 0:n], src[P:CD])]

                tasks = [[(lambda st: st[:, :, 0:INNER], Wq.rearrange("(k p) n -> p k n", p=P))],
                         halves(INNER, Wk), halves(INNER, Wv),
                         [(lambda st: st[:, :, :].rearrange("p a b -> p (a b)")[:, 0:NH * D].rearrange(
                             "p (h n) -> p h n", h=NH), Wout.rearrange("(h d) n -> d h n", d=DH))]]
                tasks += [halves(CH, ctxT[:, c * CH:(c + 1) * CH]) for c in range(NKEY // CH)]

                with nc.Block() as block:

                    @block.sync
                    def _(sp):
                        sp.dma_start(x32[:, :, :], xT.rearrange("(k p) t -> p k t", p=P)).then_inc(s_x, 16)
                        sp.dma_start(wa32[:, :, :], WA.rearrange("(k p) n -> p k n", p=P)).then_inc(s_wa, 16)
                        sp.dma_start(wo32[:, :, :], Wo.rearrange("(k p) n -> p k n", p=P)).then_inc(s_wo, 16)
                        sp.dma_start(res[:, :, :], x.rearrange("(b t) d -> t b d", t=T)).then_inc(s_res, 16)
                        for i, task in enumerate(tasks):
                            if i >= 2:
                                sp.wait_ge(s_staged, i - 1)
                            for dst, src in task:
                                sp.dma_start(dst(stage[i % 2]), src).then_inc(s_stage[i % 2], 16)

                    @block.gpsimd
                    def _(g):
                        run = chain(g, s_g)
                        run(g.memset(ident[:, :], 0.0))
                        g.affine_select(out=ident[:, :], in_=ident[:, :], compare_op=ALU.not_equal, fill=1.0,
                                        base=0, pattern=[[-1, P]], channel_multiplier=1).then_inc(s_const, 1)
                        g.memset(ones[:, :], 1.0).then_inc(s_const, 1)
                        for t in (ctx_hi, ctx_lo, ctx_s):
                            run(g.memset(t[:, NKEY:NKEY + KPAD], 0.0))
                        for n in "kv":
                            run(g.memset(wkv[n][3][64:P, :], 0.0))
                        loaded = [0, 0]
                        for i, task in enumerate(tasks):
                            st = stage[i % 2]
                            loaded[i % 2] += 16 * len(task)
                            g.wait_ge(s_stage[i % 2], loaded[i % 2])
                            if i < 4:
                                flat = st[:, :, :].rearrange("p a b -> p (a b)")[:, 0:NH * D] if i == 3 \
                                    else st[:, :, 0:INNER]
                                run(g.tensor_scalar(flat, flat, WSCALE, 1.0, ALU.mult, ALU.mult))
                            if i == 0:
                                run(g.tensor_copy(wq_hi[:, :, :], flat))
                                run(g.tensor_tensor(wq_lo[:, :, :], flat, wq_hi[:, :, :], ALU.subtract))
                            elif i in (1, 2):
                                hi, lo, s_hi, s_lo = wkv["kv"[i - 1]]
                                run(g.tensor_copy(hi[:, :], st[:, 0, 0:INNER]))
                                run(g.tensor_tensor(lo[:, :], st[:, 0, 0:INNER], hi[:, :], ALU.subtract))
                                run(g.tensor_copy(s_hi[:, :], st[:, 1, 0:INNER]))
                                run(g.tensor_tensor(s_lo[0:64, :], st[0:64, 1, 0:INNER], s_hi[0:64, :],
                                                    ALU.subtract))
                            elif i == 3:
                                hi, lo = [w[:, :, :].rearrange("p h n -> p (h n)") for w in (wout_hi, wout_lo)]
                                run(g.tensor_copy(hi, flat))
                                run(g.tensor_tensor(lo, flat, hi, ALU.subtract))
                            else:
                                c0 = (i - 4) * CH
                                hi, lo, s = [t[:, c0:c0 + CH] for t in (ctx_hi, ctx_lo, ctx_s)]
                                run(g.tensor_copy(hi, st[:, 0, 0:CH]))
                                run(g.tensor_tensor(lo, st[:, 0, 0:CH], hi, ALU.subtract))
                                run(g.tensor_copy(s, st[:, 1, 0:CH]))
                                s_low = ctx_s[64:P, c0:c0 + CH]
                                run(g.tensor_tensor(s_low, st[64:P, 1, 0:CH], s_low, ALU.subtract))
                            g.sem_inc(s_staged, 1)

                    @block.tensor
                    def _(pe):
                        pe.wait_ge(s_split, 4)
                        with pe.Fori(0, NQC) as c:
                            cols = bass.ds(c * QC, QC)
                            for j in range(NJ + 1):
                                pe.wait_ge(s_pl, c * 9 + (j + 1 if j < NJ else 8))
                                w = slice(WA_Q + j * P, WA_Q + (j + 1) * P)
                                for n, (k, wt, xt) in enumerate([(k, wt, xt) for k in range(2) for wt, xt in (
                                        (wa_hi, yT_hi), (wa_hi, yT_lo), (wa_lo, yT_hi))]):
                                    mm = pe.matmul(psum[:, j, 0:QC], lhsT=wt[:, k, w], rhs=xt[:, k, cols],
                                                   start=(n == 0), stop=(n == 5))
                                mm.then_inc(s_pj, 1)
                            pe.wait_ge(s_pl, c * 9 + 9)
                            for i in range(QC // T):
                                for n, (k, wt, xt) in enumerate([(k, wt, xt) for k in range(2) for wt, xt in (
                                        (wa_hi, yT_hi), (wa_hi, yT_lo), (wa_lo, yT_hi))]):
                                    mm = pe.matmul(psum[0:T, 5, i * 64:(i + 1) * 64],
                                                   lhsT=xt[:, k, bass.ds(c * QC + i * T, T)],
                                                   rhs=wt[:, k, WA_V:WA_N], start=(n == 0), stop=(n == 5))
                            mm.then_inc(s_pj, 1)

                        pe.wait_ge(s_pl, 9 + 9 * NQC)
                        pe.wait_ge(s_const, 2)
                        pe.wait_ge(s_wo, 16)

                        def scores(b, r):
                            u = b * 2 + r
                            pe.wait_ge(s_sub, u + 1)
                            tok = bass.ds(b * T, T)
                            for jj in range(2):
                                j = 2 * r + jj
                                for n, (q, k) in enumerate(((q_hi, kb_hi), (q_hi, kb_lo), (q_lo, kb_hi))):
                                    mm = pe.matmul(psum[0:T, j, 0:NG * T].rearrange("p (g t) -> p g t", g=NG),
                                                   lhsT=q[:, j, tok], rhs=k[:, :, tok],
                                                   start=(n == 0), stop=(n == 2))
                            mm.then_inc(s_s, 1)

                        def attend(b, r):
                            u = b * 2 + r
                            pe.wait_ge(s_exp, u + 3)
                            pe.wait_ge(s_ptc, u + 1)
                            for hh in range(8):
                                mm = pe.transpose(psum[0:T, 4 + hh // 4, (hh % 4) * T:(hh % 4 + 1) * T],
                                                  prob[r][:, hh, :], ident[0:T, 0:T])
                            mm.then_inc(s_T, 1)
                            pe.wait_ge(s_ptc, u + 2)
                            pe.wait_ge(s_nrm, u + 1)
                            for hh in range(8):
                                mm = pe.matmul(psum[0:T, 6, hh * (DH_S + 1):(hh + 1) * (DH_S + 1)],
                                               lhsT=probT[r][:, hh, :], rhs=vs[:, b, hh % NG, :],
                                               start=True, stop=True)
                            mm.then_inc(s_av, 1)

                        def project(b):
                            pe.wait_ge(s_nrm, b * 2 + 3)
                            pe.wait_ge(s_add, b + 1)
                            for k in range(2):
                                mm = pe.transpose(psum[:, 7, k * T:(k + 1) * T], att[:, k * P:(k + 1) * P],
                                                  ident[0:T, 0:T])
                            mm.then_inc(s_at, 1)
                            pe.wait_ge(s_atc, b + 1)
                            for k in range(2):
                                mm = pe.matmul(psum[0:T, 7, D:2 * D], lhsT=attT[:, k, :], rhs=wo32[:, k, :],
                                               start=(k == 0), stop=(k == 1))
                            mm.then_inc(s_wop, 1)

                        def batch(b, last):
                            scores(b, 1)
                            attend(b, 0)
                            if not last:
                                scores(b + 1, 0)
                            attend(b, 1)
                            project(b)

                        credit(pe, s_T, 2)
                        credit(pe, s_av, 2)
                        credit(pe, s_at, 1)
                        scores(0, 0)
                        with pe.Fori(0, NB - 1) as b:
                            batch(b, False)
                        batch(NB - 1, True)

                    @block.scalar
                    def _(a):
                        with a.Fori(0, NQC) as c:
                            cols = bass.ds(c * QC, QC)
                            for j in range(NJ):
                                a.wait_ge(s_pj, c * 6 + j + 1)
                                a.activation(q_hi[:, j, cols], psum[:, j, 0:QC], ACT.Copy,
                                             scale=1 / WSCALE).then_inc(s_ph, 1)
                            a.wait_ge(s_pj, c * 6 + NJ + 1)
                            a.wait_ge(s_prep, 2)
                            for g in range(NG):
                                rows32 = slice(g * DPAD, (g + 1) * DPAD)
                                a.activation(kb_hi[rows32, g, cols], psum[rows32, NJ, 0:QC], ACT.Copy,
                                             scale=1 / WSCALE).then_inc(s_ph, 1)

                        def exps(b, r):
                            u = b * 2 + r
                            a.wait_ge(s_sub, u + 3)
                            a.wait_ge(s_T, u + 1)
                            a.activation(prob[r][:, :, :], shifted[r][:, :, :], ACT.Exp,
                                         scale=DH_S ** -0.5).then_inc(s_exp, 1)

                        def copy_probT(b, r):
                            u = b * 2 + r
                            a.wait_ge(s_T, u + 3)
                            a.wait_ge(s_av, u + 1)
                            a.activation(probT[r][:, :, :].rearrange("p (c h) t -> p c (h t)", c=2),
                                         psum[0:T, 4:6, 0:4 * T], ACT.Copy).then_inc(s_ptc, 1)

                        def batch(b, last):
                            exps(b, 1)
                            copy_probT(b, 0)
                            if not last:
                                exps(b + 1, 0)
                            copy_probT(b, 1)
                            a.wait_ge(s_at, b + 2)
                            a.activation(attT[:, :, :], psum[:, 7, 0:2 * T].rearrange("p (k t) -> p k t", k=2),
                                         ACT.Copy).then_inc(s_atc, 1)

                        credit(a, s_ptc, 1)
                        credit(a, s_exp, 2)
                        exps(0, 0)
                        with a.Fori(0, NB - 1) as b:
                            batch(b, False)
                        batch(NB - 1, True)

                    @block.vector
                    def _(v):
                        v.memset(kb_hi[:, :, :].bitcast(F32), 0.0).then_inc(s_prep, 1)
                        v.memset(kb_lo[:, :, :].bitcast(F32), 0.0).then_inc(s_prep, 1)
                        v.memset(vs[:, :, :, :], 1.0).then_inc(s_prep, 1)
                        v.wait_ge(s_x, 16)
                        v.tensor_copy(yT_hi[:, :, :], x32[:, :, :]).then_inc(s_split, 1)
                        v.wait_ge(s_wa, 16)
                        v.tensor_scalar(wa_hi[:, :, :], wa32[:, :, :], WSCALE, None, ALU.mult).then_inc(s_split, 1)
                        v.wait_ge(s_split, 2)
                        v.tensor_tensor(yT_lo[:, :, :], x32[:, :, :], yT_hi[:, :, :],
                                        ALU.subtract).then_inc(s_split, 1)
                        v.scalar_tensor_tensor(wa_lo[:, :, :], wa32[:, :, :], WSCALE, wa_hi[:, :, :],
                                               ALU.mult, ALU.subtract).then_inc(s_split, 1)
                        credit(v, s_pl, 9)
                        v.wait_ge(s_prep, 3)
                        with v.Fori(0, NQC) as c:
                            cols = bass.ds(c * QC, QC)
                            for j in range(NJ):
                                v.wait_ge(s_ph, c * 8 + j + 1)
                                v.scalar_tensor_tensor(q_lo[:, j, cols], psum[:, j, 0:QC], 1 / WSCALE,
                                                       q_hi[:, j, cols], ALU.mult, ALU.subtract).then_inc(s_pl, 1)
                            for g in range(NG):
                                rows32 = slice(g * DPAD, (g + 1) * DPAD)
                                v.wait_ge(s_ph, c * 8 + NJ + g + 1)
                                v.scalar_tensor_tensor(kb_lo[rows32, g, cols], psum[rows32, NJ, 0:QC], 1 / WSCALE,
                                                       kb_hi[rows32, g, cols], ALU.mult,
                                                       ALU.subtract).then_inc(s_pl, 1)
                            v.wait_ge(s_pj, c * 6 + 6)
                            v.tensor_scalar(vs[:, bass.ds(c * 4, 4), :, 0:DH_S],
                                            psum[0:T, 5, 0:256].rearrange("p (b g d) -> p b g d", b=4, g=NG),
                                            1 / WSCALE, None, ALU.mult).then_inc(s_pl, 1)

                        def shift(b, r):
                            u = b * 2 + r
                            sc = psum[0:T, 2 * r:2 * r + 2, 0:4 * T].rearrange("p c (h t) -> p c h t", h=4)
                            v.wait_ge(s_s, u + 1)
                            v.wait_ge(s_exp, u + 1)
                            v.tensor_reduce(mx[r][:, :].rearrange("p (c h) -> p c h", c=2), sc, AX.X,
                                            ALU.max).then_inc(s_mx, 1)
                            v.wait_ge(s_mx, u + 1)
                            for c in range(2):
                                ins = v.tensor_tensor(
                                    shifted[r][:, 4 * c:4 * c + 4, :],
                                    psum[0:T, 2 * r + c, 0:4 * T].rearrange("p (h t) -> p h t", h=4),
                                    mx[r][:, 4 * c:4 * c + 4].unsqueeze(2).broadcast_to([T, 4, T]), ALU.subtract)
                            ins.then_inc(s_sub, 1)

                        def normalise(b, r):
                            u = b * 2 + r
                            av = psum[0:T, 6, 0:8 * (DH_S + 1)].rearrange("p (h w) -> p h w", h=8)
                            v.wait_ge(s_av, u + 3)
                            v.reciprocal(rden[:, :], av[:, :, DH_S]).then_inc(s_rd, 1)
                            v.wait_ge(s_at, b + 1)
                            v.wait_ge(s_rd, u + 1)
                            heads = att[:, :].rearrange("p (g j d) -> p j g d", g=NG, j=NJ)
                            for jj in range(2):
                                ins = v.tensor_tensor(
                                    heads[:, 2 * r + jj, :, :], av[:, 4 * jj:4 * jj + 4, 0:DH_S],
                                    rden[:, 4 * jj:4 * jj + 4].unsqueeze(2).broadcast_to([T, 4, DH_S]), ALU.mult)
                            ins.then_inc(s_nrm, 1)

                        def batch(b, last):
                            shift(b, 1)
                            normalise(b, 0)
                            if not last:
                                shift(b + 1, 0)
                            normalise(b, 1)
                            v.wait_ge(s_wop, b + 1)
                            v.tensor_tensor(res[:, b, :], psum[0:T, 7, D:2 * D], res[:, b, :],
                                            ALU.add).then_inc(s_add, 1)
                            v.wait_ge(s_add, b + 2)
                            v.bn_stats(stats[:, b, :], res[:, b, :]).then_inc(s_bn, 1)

                        credit(v, s_sub, 2)
                        credit(v, s_nrm, 1)
                        credit(v, s_add, 1)
                        v.wait_ge(s_res, 16)
                        shift(0, 0)
                        with v.Fori(0, NB - 1) as b:
                            batch(b, False)
                        batch(NB - 1, True)

            layer_norm("ln1_")

            with ExitStack() as pb:
                k_hi = sb(pb, "k_hi", [P, NKEY + KPAD], F16)
                k_lo = sb(pb, "k_lo", [P, NKEY + KPAD], F16)
                v_all = sb(pb, "v_all", [P, NKT, VW], F16)
                q_hi = sb(pb, "qx_hi", [P, NT], F16)
                q_lo = sb(pb, "qx_lo", [P, NT], F16)
                shifted = [sb(pb, f"sx{r}", [P, GT, QB], F32) for r in range(2)]
                e32 = [sb(pb, f"e32_{r}", [P, GT, QB], F32) for r in range(2)]
                e_hi = [sb(pb, f"e_hi{r}", [P, GT, QB], F16) for r in range(2)]
                e_lo = [sb(pb, f"e_lo{r}", [P, GT, QB], F16) for r in range(2)]
                part_max = sb(pb, "part_max", [P, QT, NKC], F32)
                row_max = sb(pb, "row_max", [P, QT], F32)
                diag = sb(pb, "diag", [P, QB], F32)
                max_b = sb(pb, "max_b", [P, QB], F32)
                o_buf = sb(pb, "o_buf", [P, QT, VW], F32)

                (s_init, s_pj, s_ph, s_pl, s_qk, s_sub, s_e, s_hi, s_lo, s_av, s_oev, s_od, s_mxp, s_red,
                 s_rm, s_dg, s_bc, s_mb) = [sem("b_" + n) for n in (
                     "init", "pj", "ph", "pl", "qk", "sub", "e", "hi", "lo", "av", "oev", "od", "mxp", "red",
                     "rm", "dg", "bc", "mb")]
                TASKS = NKC + NQC + NGRP
                HG = NQB * NGRP

                with nc.Block() as block:

                    @block.tensor
                    def _(pe):
                        def scores(f, step, q0, r):
                            pe.wait_ge(s_sub, f + 1)
                            for i in range(GT):
                                keys = bass.ds((step * GT + i) * KT, P)
                                for n, (k, q) in enumerate(((k_hi, q_hi), (k_hi, q_lo), (k_lo, q_hi))):
                                    mm = pe.matmul(psum[:, 2 * r + i // 2, (i % 2) * QB:(i % 2 + 1) * QB],
                                                   lhsT=k[:, keys], rhs=q[:, bass.ds(q0, QB)],
                                                   start=(n == 0), stop=(n == 2))
                            mm.then_inc(s_qk, 1)

                        def attend(f, step, r, first=False, last=False):
                            pe.wait_ge(s_lo, f + 3)
                            for i in range(GT):
                                for t in range(QT):
                                    q = slice(t * P, (t + 1) * P)
                                    hi = (e_hi, VW)
                                    lo = (e_lo, DH + 1)
                                    start, stop = first and i == 0, last and i == GT - 1
                                    for n, (e, w) in enumerate((lo, hi) if stop else (hi, lo)):
                                        mm = pe.matmul(psum[:, 4 + t, 0:w], lhsT=e[r][0:KT, i, q],
                                                       rhs=v_all[0:KT, step * GT + i, 0:w],
                                                       start=start and n == 0, stop=stop and n == 1)
                            mm.then_inc(s_av, 1)

                        def max_piece(n, p, q0):
                            pe.wait_ge(s_red, n * NKC + p + 1)
                            for t in range(QT):
                                mm = pe.matmul(psum[:, 6 + t, 0:KC], lhsT=q_hi[:, bass.ds(q0 + t * P, P)],
                                               rhs=k_hi[:, bass.ds(p * KC, KC)], start=True, stop=True)
                            mm.then_inc(s_mxp, 1)

                        def spread_max(n):
                            pe.wait_ge(s_dg, n + 1)
                            pe.matmul(psum[:, 6, 0:QB], lhsT=ones[:, :], rhs=diag[:, :],
                                      start=True, stop=True).then_inc(s_bc, 1)

                        def block_steps(h, qb, last):
                            n = h * NQB + qb
                            f0 = n * NGRP
                            q0, q1 = qb * QB, qb * QB + QB
                            pe.wait_ge(s_oev, n + 1)
                            if not last:
                                pe.wait_ge(s_mb, n + 2)
                            for s in range(2):
                                scores(f0 + s + 2, s + 2, q0, s)
                                attend(f0 + s, s, s, first=(s == 0))
                                if not last:
                                    max_piece(n + 1, 2 * s, q1)
                                    max_piece(n + 1, 2 * s + 1, q1)
                            with counted(pe, 2, NGRP - 2, 2) as s:
                                for r in range(2):
                                    scores(f0 + s + (r + 2), s + (r + 2), q0, r)
                                    attend(f0 + s + r, s + r, r)
                                    if not last:
                                        max_piece(n + 1, s + (r + 2), q1)
                            if not last:
                                scores(f0 + NGRP, 0, q1, 0)
                                spread_max(n + 1)
                            attend(f0 + NGRP - 2, NGRP - 2, 0)
                            if not last:
                                scores(f0 + NGRP + 1, 1, q1, 1)
                            attend(f0 + NGRP - 1, NGRP - 1, 1, last=True)

                        credit(pe, s_av, 2)
                        pe.wait_ge(s_init, 4)
                        with pe.Fori(0, NH) as h:
                            hd = bass.ds(h * DH, DH)
                            with counted(pe, 0, NKC, 4) as c:
                                pe.wait_ge(s_sub, h * HG + 2)
                                for r in range(4):
                                    pe.wait_ge(s_pl, h * TASKS + c + (r + 1))
                                    whi, wlo, wshi, wslo = wkv["k"]
                                    for n, (w, x_) in enumerate(((whi, ctx_hi), (whi, ctx_lo), (wlo, ctx_hi),
                                                                 (wshi, ctx_s), (wslo, ctx_s))):
                                        mm = pe.matmul(psum[:, r, 0:KC], lhsT=w[:, hd],
                                                       rhs=x_[:, bass.ds((c + r) * KC, KC)],
                                                       start=(n == 0), stop=(n == 4))
                                    mm.then_inc(s_pj, 1)
                            for c in range(NQC):
                                pe.wait_ge(s_pl, h * TASKS + NKC + c + 1)
                                for n, (k, w, x_) in enumerate([(k, w, x_) for k in range(2) for w, x_ in (
                                        (wq_hi, yT_hi), (wq_hi, yT_lo), (wq_lo, yT_hi))]):
                                    mm = pe.matmul(psum[:, c, 0:QC], lhsT=w[:, k, hd],
                                                   rhs=x_[:, k, c * QC:(c + 1) * QC],
                                                   start=(n == 0), stop=(n == 5))
                                mm.then_inc(s_pj, 1)
                            with counted(pe, 0, NGRP, 4) as c:
                                pe.wait_ge(s_pl, h * TASKS + NKC + NQC + 4)
                                pe.wait_ge(s_mb, h * NQB + 1)
                                for r in range(4):
                                    max_piece(h * NQB, c + r, 0)
                                    pe.wait_ge(s_pl, h * TASKS + NKC + NQC + c + (r + 1))
                                    whi, wlo, wshi, wslo = wkv["v"]
                                    for i in range(GT):
                                        keys = bass.ds(((c + r) * GT + i) * KT, P)
                                        for n, (x_, w) in enumerate(((ctx_hi, whi), (ctx_hi, wlo), (ctx_lo, whi),
                                                                     (ctx_s, wshi), (ctx_s, wslo))):
                                            mm = pe.matmul(psum[:, r, i * DH:(i + 1) * DH], lhsT=x_[:, keys],
                                                           rhs=w[:, hd], start=(n == 0), stop=(n == 4))
                                    mm.then_inc(s_pj, 1)
                            spread_max(h * NQB)
                            pe.wait_ge(s_pl, h * TASKS + TASKS + 4)
                            scores(h * HG, 0, 0, 0)
                            scores(h * HG + 1, 1, 0, 1)
                            with pe.Fori(0, NQB - 1) as qb:
                                block_steps(h, qb, False)
                            block_steps(h, NQB - 1, True)

                    @block.scalar
                    def _(a):
                        def exps(f, r):
                            a.wait_ge(s_sub, f + 3)
                            a.wait_ge(s_lo, f + 1)
                            a.activation(e32[r][0:KT, :, :], shifted[r][0:KT, :, :], ACT.Exp,
                                         scale=SIM_SCALE).then_inc(s_e, 1)
                            a.wait_ge(s_av, f + 1)
                            a.activation(e_hi[r][0:KT, :, :], shifted[r][0:KT, :, :], ACT.Exp,
                                         scale=SIM_SCALE).then_inc(s_hi, 1)

                        def block_steps(h, qb, last):
                            n = h * NQB + qb
                            f0 = n * NGRP
                            with counted(a, 2, NGRP if last else NGRP + 2, 2) as s:
                                for r in range(2):
                                    exps(f0 + s + r, r)
                            a.wait_ge(s_av, f0 + NGRP + 2)
                            a.wait_ge(s_od, n * 16 + 16)
                            a.activation(o_buf[:, :, :], psum[:, 4:6, 0:VW], ACT.Copy).then_inc(s_oev, 1)

                        credit(a, s_hi, 2)
                        credit(a, s_oev, 1)
                        with a.Fori(0, NH) as h:
                            with counted(a, 0, NKC, 4) as c:
                                for r in range(4):
                                    a.wait_ge(s_pj, h * TASKS + c + (r + 1))
                                    a.activation(k_hi[:, bass.ds((c + r) * KC, KC)], psum[:, r, 0:KC], ACT.Copy,
                                                 scale=1 / WSCALE).then_inc(s_ph, 1)
                            for c in range(NQC):
                                a.wait_ge(s_pj, h * TASKS + NKC + c + 1)
                                a.activation(q_hi[:, c * QC:(c + 1) * QC], psum[:, c, 0:QC], ACT.Copy,
                                             scale=1 / WSCALE).then_inc(s_ph, 1)
                            with counted(a, 0, NGRP, 4) as c:
                                for r in range(4):
                                    a.wait_ge(s_pj, h * TASKS + NKC + NQC + c + (r + 1))
                                    a.activation(v_all[0:KT, bass.ds((c + r) * GT, GT), 0:DH],
                                                 psum[0:KT, r, :].rearrange("p (i d) -> p i d", i=GT), ACT.Copy,
                                                 scale=1 / WSCALE).then_inc(s_ph, 1)
                            for r in range(2):
                                exps(h * HG + r, r)
                            with a.Fori(0, NQB - 1) as qb:
                                block_steps(h, qb, False)
                            block_steps(h, NQB - 1, True)

                    @block.vector
                    def _(v):
                        def shift(f, r):
                            v.wait_ge(s_qk, f + 1)
                            v.wait_ge(s_hi, f + 1)
                            for c in range(2):
                                ins = v.tensor_tensor(
                                    shifted[r][0:KT, 2 * c:2 * c + 2, :],
                                    psum[0:KT, 2 * r + c, :].rearrange("p (i q) -> p i q", i=2),
                                    max_b[0:KT, :].unsqueeze(1).broadcast_to([KT, 2, QB]), ALU.subtract)
                            ins.then_inc(s_sub, 1)

                        def reduce_piece(n, p):
                            v.wait_ge(s_mxp, n * NKC + p + 1)
                            v.tensor_reduce(part_max[:, :, bass.ds(p, 1)] if not isinstance(p, int)
                                            else part_max[:, :, p:p + 1],
                                            psum[:, 6:8, 0:KC], AX.X, ALU.max).then_inc(s_red, 1)

                        def finish_max(n):
                            v.wait_ge(s_red, n * NKC + NKC + 1)
                            v.tensor_reduce(row_max[:, :], part_max[:, :, :], AX.X, ALU.max).then_inc(s_rm, 1)
                            v.wait_ge(s_rm, n + 1)
                            v.tensor_tensor(diag[:, :].rearrange("p (t q) -> p t q", t=QT),
                                            ident[:, :].unsqueeze(1).broadcast_to([P, QT, P]),
                                            row_max[:, :].unsqueeze(2).broadcast_to([P, QT, P]),
                                            ALU.mult).then_inc(s_dg, 1)
                            v.wait_ge(s_bc, n + 1)
                            v.tensor_scalar(max_b[:, :], psum[:, 6, 0:QB], -LIFT, None, ALU.add).then_inc(s_mb, 1)
                            v.wait_ge(s_mb, n + 2)

                        def block_steps(h, qb, last):
                            n = h * NQB + qb
                            f0 = n * NGRP
                            for s in range(2):
                                shift(f0 + s + 2, s)
                                if not last:
                                    reduce_piece(n + 1, 2 * s)
                                    reduce_piece(n + 1, 2 * s + 1)
                            with counted(v, 2, NGRP - 2, 2) as s:
                                for r in range(2):
                                    shift(f0 + s + (r + 2), r)
                                    if not last:
                                        reduce_piece(n + 1, s + (r + 2))
                            if not last:
                                finish_max(n + 1)
                                shift(f0 + NGRP, 0)
                                shift(f0 + NGRP + 1, 1)

                        credit(v, s_sub, 2)
                        credit(v, s_pl, 4)
                        credit(v, s_red, 1)
                        credit(v, s_mb, 1)
                        v.memset(k_hi[:, NKEY:NKEY + KPAD], 0.0).then_inc(s_init, 1)
                        v.memset(k_lo[:, NKEY:NKEY + KPAD], 0.0).then_inc(s_init, 1)
                        v.memset(v_all[:, :, DH:DH + 1], 1.0).then_inc(s_init, 1)
                        v.memset(part_max[:, :, :], 0.0).then_inc(s_init, 1)
                        v.wait_ge(s_init, 4)
                        with v.Fori(0, NH) as h:
                            with counted(v, 0, NKC, 4) as c:
                                for r in range(4):
                                    cols = bass.ds((c + r) * KC, KC)
                                    v.wait_ge(s_ph, h * TASKS + c + (r + 1))
                                    v.scalar_tensor_tensor(k_lo[:, cols], psum[:, r, 0:KC], 1 / WSCALE,
                                                           k_hi[:, cols], ALU.mult, ALU.subtract).then_inc(s_pl, 1)
                            for c in range(NQC):
                                cols = slice(c * QC, (c + 1) * QC)
                                v.wait_ge(s_ph, h * TASKS + NKC + c + 1)
                                v.scalar_tensor_tensor(q_lo[:, cols], psum[:, c, 0:QC], 1 / WSCALE,
                                                       q_hi[:, cols], ALU.mult, ALU.subtract).then_inc(s_pl, 1)
                            with counted(v, 0, NGRP, 4) as c:
                                for r in range(4):
                                    reduce_piece(h * NQB, c + r)
                                    tiles4 = bass.ds((c + r) * GT, GT)
                                    v.wait_ge(s_ph, h * TASKS + NKC + NQC + c + (r + 1))
                                    v.scalar_tensor_tensor(
                                        v_all[0:KT, tiles4, DH + 1:VW],
                                        psum[0:KT, r, :].rearrange("p (i d) -> p i d", i=GT), 1 / WSCALE,
                                        v_all[0:KT, tiles4, 0:DH], ALU.mult, ALU.subtract).then_inc(s_pl, 1)
                            finish_max(h * NQB)
                            for r in range(2):
                                shift(h * HG + r, r)
                            with v.Fori(0, NQB - 1) as qb:
                                block_steps(h, qb, False)
                            block_steps(h, NQB - 1, True)

                    @block.gpsimd
                    def _(g):
                        credit(g, s_lo, 2)
                        with counted(g, 0, NH * HG, 2) as f:
                            for r in range(2):
                                g.wait_ge(s_hi, f + (r + 3))
                                g.tensor_tensor(e_lo[r][0:KT, :, :], e32[r][0:KT, :, :], e_hi[r][0:KT, :, :],
                                                ALU.subtract).then_inc(s_lo, 1)

                    @block.sync
                    def _(sp):
                        credit(sp, s_od, 16)
                        with sp.Fori(0, NH) as h:
                            with sp.Fori(0, NQB) as qb:
                                sp.wait_ge(s_oev, h * NQB + qb + 2)
                                sp.dma_start(o_dram[bass.ds(qb * QB, QB), bass.ds(h * VW, VW)].rearrange(
                                    "(t p) w -> p t w", p=P), o_buf[:, :, :]).then_inc(s_od, 16)
                        sp.wait_ge(s_od, NH * NQB * 16 + 16)

        with ExitStack() as cd:
            w1t = sb(cd, "w1t", [P, 2, FF], F16)
            w2t = sb(cd, "w2t", [P, FF // P, D], F16)
            b1s = sb(cd, "b1s", [P, FF // P], F32)
            bout_b = sb(cd, "bout_b", [T, D], F32)
            b2_b = sb(cd, "b2_b", [T, D], F32)

            with ExitStack() as pc:
                w32 = [sb(pc, f"w32_{i}", [P, 2 * FF], F32) for i in range(2)]
                below = sb(pc, "below", [P, 2 * FF], F32)
                thr = [sb(pc, f"thr{i}", [P, 2], F32) for i in range(2)]
                sum_p = sb(pc, "sum_p", [P, 2], F32)
                raw = [sb(pc, f"raw{r}", [T, NH, VW], F32) for r in range(2)]
                o_sum = [sb(pc, f"o_sum{r}", [T, NH, DH], F32) for r in range(2)]
                rden = [sb(pc, f"rden_c{r}", [T, NH], F32) for r in range(2)]
                oT_hi = [sb(pc, f"oT_hi{r}", [P, NH, T], F16) for r in range(2)]
                oT_lo = [sb(pc, f"oT_lo{r}", [P, NH, T], F16) for r in range(2)]

                s_w, s_bias, s_b1, s_b2 = sem("c_w"), sem("c_bias"), sem("c_b1"), sem("c_b2")
                s_raw = [sem(f"c_raw{r}") for r in range(2)]
                (s_ab, s_tot, s_t, s_seed, s_rd, s_sum, s_on, s_tr, s_hi, s_lo, s_wp, s_add, s_bn) = [
                    sem("c_" + n) for n in ("ab", "tot", "t", "seed", "rd", "sum", "on", "tr", "hi", "lo",
                                            "wp", "add", "bn")]
                with nc.Block() as block:

                    @block.sync
                    def _(sp):
                        sp.dma_start(w32[0][:, :].rearrange("p (k n) -> p k n", k=2),
                                     W1T.rearrange("(k p) n -> p k n", p=P)).then_inc(s_w, 16)
                        sp.dma_start(w32[1][:, :].rearrange("p (k n) -> p k n", k=FF // P),
                                     W2T.rearrange("(k p) n -> p k n", p=P)).then_inc(s_w, 16)
                        sp.dma_start(bout_b[:, :], bout.unsqueeze(0).broadcast_to([T, D])).then_inc(s_bias, 16)
                        sp.dma_start(b2_b[:, :], b2.unsqueeze(0).broadcast_to([T, D])).then_inc(s_b2, 16)
                        sp.dma_start(b1s[:, :], b1).then_inc(s_b1, 16)
                        with counted(sp, 0, NB, 2) as b:
                            for r in range(2):
                                sp.wait_ge(s_on, b + (r + 1))
                                sp.dma_start(raw[r][:, :, :].rearrange("p h w -> p (h w)"),
                                             o_dram[bass.ds((b + r) * T, T), :]).then_inc(s_raw[r], 16)
                        sp.wait_ge(s_b2, 16)
                        sp.wait_ge(s_b1, 16)

                    @block.gpsimd
                    def _(g):
                        g.wait_ge(s_bias, 16)
                        with g.Fori(0, NB) as b:
                            g.tensor_tensor(res[:, b, :], res[:, b, :], bout_b[:, :], ALU.add).then_inc(s_seed, 1)
                        with counted(g, 0, NB, 2) as b:
                            for r in range(2):
                                g.wait_ge(s_raw[r], b * 8 + 16)
                                g.wait_ge(s_tr, b + (r + 1))
                                g.tensor_tensor(o_sum[r][:, :, :], raw[r][:, :, 0:DH], raw[r][:, :, DH + 1:VW],
                                                ALU.add).then_inc(s_sum, 1)

                    @block.vector
                    def _(v):
                        v.wait_ge(s_w, 32)
                        for i in range(2):
                            v.tensor_reduce(sum_p[:, i:i + 1], w32[i][:, :], AX.X, ALU.add,
                                            apply_absolute_value=True).then_inc(s_ab, 1)
                        v.wait_ge(s_tot, 1)
                        for i in range(2):
                            n = i * 4
                            v.tensor_scalar(thr[i][:, 0:1], psum[:, 7, i:i + 1], 1.0 / (D * FF), 1e-8,
                                            ALU.mult, ALU.max).then_inc(s_t, 1)
                            v.wait_ge(s_t, n + 1)
                            v.tensor_scalar(thr[i][:, 1:2], thr[i][:, 0:1], -0.5, None, ALU.mult).then_inc(s_t, 1)
                            v.wait_ge(s_t, n + 2)
                            v.tensor_scalar(thr[i][:, 0:1], thr[i][:, 0:1], 0.5, None, ALU.mult).then_inc(s_t, 1)
                            v.wait_ge(s_t, n + 3)
                            v.tensor_scalar(below[:, :], w32[i][:, :], thr[i][:, 1:2], None,
                                            ALU.is_lt).then_inc(s_t, 1)
                            v.wait_ge(s_t, n + 4)
                            wt = (w1t, w2t)[i][:, :, :].rearrange("p k n -> p (k n)")
                            v.scalar_tensor_tensor(wt, w32[i][:, :], thr[i][:, 0:1], below[:, :],
                                                   ALU.is_gt, ALU.subtract).then_inc(s_ab, 1)

                        def normalise(b, r):
                            v.wait_ge(s_raw[r], b * 8 + 16)
                            v.reciprocal(rden[r][:, :], raw[r][:, :, DH]).then_inc(s_rd, 1)
                            v.wait_ge(s_rd, b + (r + 1))
                            v.wait_ge(s_sum, b + (r + 1))
                            v.tensor_tensor(o_sum[r][:, :, :], o_sum[r][:, :, :],
                                            rden[r][:, :].unsqueeze(2).broadcast_to([T, NH, DH]),
                                            ALU.mult).then_inc(s_on, 1)

                        def low(b, r):
                            v.wait_ge(s_hi, b + (r + 1))
                            v.tensor_tensor(oT_lo[r][:, :, :].rearrange("p (c h) t -> p c (h t)", c=2),
                                            psum[:, 2 * r:2 * r + 2, 0:4 * T],
                                            oT_hi[r][:, :, :].rearrange("p (c h) t -> p c (h t)", c=2),
                                            ALU.subtract).then_inc(s_lo, 1)

                        def residual(b, r):
                            v.wait_ge(s_wp, b + (r + 3))
                            v.scalar_tensor_tensor(res[:, b + r, :], psum[0:T, 4 + r, 0:D], 1 / WSCALE,
                                                   res[:, b + r, :], ALU.mult, ALU.add).then_inc(s_add, 1)
                            v.wait_ge(s_add, b + (r + 3))
                            v.bn_stats(stats[:, b + r, :], res[:, b + r, :]).then_inc(s_bn, 1)

                        credit(v, s_lo, 2)
                        credit(v, s_on, 2)
                        credit(v, s_add, 2)
                        v.wait_ge(s_seed, NB)
                        with counted(v, 0, NB, 2) as b:
                            for r in range(2):
                                normalise(b, r)
                            for r in range(2):
                                low(b, r)
                            for r in range(2):
                                residual(b, r)

                    @block.scalar
                    def _(a):
                        with counted(a, 0, NB, 2) as b:
                            for r in range(2):
                                a.wait_ge(s_tr, b + (r + 3))
                                a.wait_ge(s_wp, b + (r + 1))
                                a.activation(oT_hi[r][:, :, :].rearrange("p (c h) t -> p c (h t)", c=2),
                                             psum[:, 2 * r:2 * r + 2, 0:4 * T], ACT.Copy).then_inc(s_hi, 1)

                    @block.tensor
                    def _(pe):
                        pe.wait_ge(s_ab, 2)
                        pe.matmul(psum[:, 7, 0:2], lhsT=ones[:, :], rhs=sum_p[:, :],
                                  start=True, stop=True).then_inc(s_tot, 1)
                        credit(pe, s_tr, 2)
                        credit(pe, s_wp, 2)
                        with counted(pe, 0, NB, 2) as b:
                            for r in range(2):
                                pe.wait_ge(s_on, b + (r + 3))
                                pe.wait_ge(s_lo, b + (r + 1))
                                for h in range(NH):
                                    mm = pe.transpose(psum[:, 2 * r + h // 4, (h % 4) * T:(h % 4 + 1) * T],
                                                      o_sum[r][:, h, :], ident[0:T, 0:T])
                                mm.then_inc(s_tr, 1)
                            for r in range(2):
                                pe.wait_ge(s_lo, b + (r + 3))
                                pe.wait_ge(s_add, b + (r + 1))
                                for n, (h, o, w) in enumerate([(h, o, w) for h in range(NH) for o, w in (
                                        (oT_hi, wout_hi), (oT_hi, wout_lo), (oT_lo, wout_hi))]):
                                    mm = pe.matmul(psum[0:T, 4 + r, 0:D], lhsT=o[r][:, h, :], rhs=w[:, h, :],
                                                   start=(n == 0), stop=(n == 3 * NH - 1))
                                mm.then_inc(s_wp, 1)

            layer_norm("ln2_")

            with ExitStack() as pd:
                h32 = [sb(pd, f"h32_{r}", [P, QC], F32) for r in range(2)]
                hT_hi = sb(pd, "hT_hi", [P, FF // P, QC], F16)
                hT_lo = sb(pd, "hT_lo", [P, FF // P, QC], F16)
                (s_f1, s_ge, s_hh, s_hl, s_f2, s_seed, s_add, s_bn) = [
                    sem("d_" + n) for n in ("f1", "ge", "hh", "hl", "f2", "seed", "add", "bn")]
                NF, NI = FF // P, QC // T
                with nc.Block() as block:

                    @block.tensor
                    def _(pe):
                        credit(pe, s_f2, NI)
                        with pe.Fori(0, NQC) as c:
                            cols = bass.ds(c * QC, QC)
                            for f in range(NF):
                                pe.wait_ge(s_ge, c * NF + f + 1)
                                for n, (k, y) in enumerate([(k, y) for k in range(2) for y in (yT_hi, yT_lo)]):
                                    mm = pe.matmul(psum[:, f % 4, 0:QC], lhsT=w1t[:, k, f * P:(f + 1) * P],
                                                   rhs=y[:, k, cols], start=(n == 0), stop=(n == 3))
                                mm.then_inc(s_f1, 1)
                            pe.wait_ge(s_hl, c * NF + NF + 2)
                            for i in range(NI):
                                pe.wait_ge(s_add, c * NI + i + 1)
                                for n, (f, y) in enumerate([(f, y) for f in range(NF) for y in (hT_hi, hT_lo)]):
                                    mm = pe.matmul(psum[0:T, 4 + i, 0:D], lhsT=y[:, f, i * T:(i + 1) * T],
                                                   rhs=w2t[:, f, :], start=(n == 0), stop=(n == 2 * NF - 1))
                                mm.then_inc(s_f2, 1)

                    @block.scalar
                    def _(a):
                        credit(a, s_ge, 4)
                        with a.Fori(0, NQC) as c:
                            for f in range(NF):
                                a.wait_ge(s_f1, c * NF + f + 1)
                                a.wait_ge(s_hl, c * NF + f + 1)
                                a.activation(h32[f % 2][:, :], psum[:, f % 4, 0:QC], ACT.Gelu,
                                             bias=b1s[:, f:f + 1]).then_inc(s_ge, 1)

                    @block.vector
                    def _(v):
                        credit(v, s_hl, 2)
                        credit(v, s_add, 4)
                        v.wait_ge(s_seed, NB)
                        with v.Fori(0, NQC) as c:
                            v.wait_ge(s_f2, c * NI + NI)
                            for f in range(NF):
                                v.wait_ge(s_ge, c * NF + f + 5)
                                v.tensor_copy(hT_hi[:, f, :], h32[f % 2][:, :]).then_inc(s_hh, 1)
                                v.wait_ge(s_hh, c * NF + f + 1)
                                v.tensor_tensor(hT_lo[:, f, :], h32[f % 2][:, :], hT_hi[:, f, :],
                                                ALU.subtract).then_inc(s_hl, 1)
                            for i in range(NI):
                                v.wait_ge(s_f2, c * NI + NI + i + 1)
                                v.tensor_tensor(res[:, c * NI + i, :], psum[0:T, 4 + i, 0:D],
                                                res[:, c * NI + i, :], ALU.add).then_inc(s_add, 1)
                                v.wait_ge(s_add, c * NI + i + 5)
                                v.bn_stats(stats[:, c * NI + i, :], res[:, c * NI + i, :]).then_inc(s_bn, 1)

                    @block.gpsimd
                    def _(g):
                        with g.Fori(0, NB) as b:
                            g.tensor_tensor(res[:, b, :], res[:, b, :], b2_b[:, :], ALU.add).then_inc(s_seed, 1)

            layer_norm("ln3_", to_dram=True)


def kernel(**inputs):
    import numpy as np
    import concourse.bacc as bacc
    from concourse.bass_utils import run_bass_kernel_spmd

    i = {name: np.asarray(a) for name, a in inputs.items()}
    wq = i["L0_attn_Wq"].reshape(D, NG, NJ, DH_S).transpose(0, 2, 1, 3)
    wk = i["L0_attn_Wk"].reshape(D, NG, DH_S)
    pad = DPAD - DH_S
    wq = np.pad(wq, ((0, 0), (0, 0), (0, 0), (0, pad))).reshape(D, NJ * P)
    wk = np.pad(wk, ((0, 0), (0, 0), (0, pad))).reshape(D, P)
    laid = {
        "xT": i["x"].reshape(NT, D).T, "x": i["x"].reshape(NT, D),
        "WA": np.concatenate([wq, wk, i["L0_attn_Wv"]], axis=1), "Wo": i["L0_attn_Wo"],
        "ctxT": i["ctx_768"].reshape(NKEY, CD).T,
        "Wq": i["L0_xattn_Wq"], "Wk": i["L0_xattn_Wk"], "Wv": i["L0_xattn_Wv"],
        "Wout": i["L0_xattn_Wout"], "bout": i["L0_xattn_bout"],
        "W1T": i["L0_ffn_W1"].T, "b1": i["L0_ffn_b1"].reshape(FF // P, P).T, "W2T": i["L0_ffn_W2"].T, "b2": i["L0_ffn_b2"],
    }
    nc = bacc.Bacc("TRN2", target_bir_lowering=False, num_devices=1)
    arrays, args = {}, {}
    for name, a in laid.items():
        arrays["in_" + name] = np.ascontiguousarray(a)
        args[name] = nc.dram_tensor("in_" + name, a.shape, mybir.dt.from_np(a.dtype), kind="ExternalInput").ap()
    o_dram = nc.dram_tensor("o_scratch", (NT, NH * VW), F32, kind="Internal").ap()
    out = nc.dram_tensor("out_dram", (NT, D), F32, kind="ExternalOutput").ap()
    build(nc, **args, o_dram=o_dram, out=out)
    r = run_bass_kernel_spmd(nc, [arrays], core_ids=[0])
    return r.results[0]["out_dram"].reshape(NB, T, D)
```

```python
from contextlib import ExitStack

import concourse.bass as bass
from concourse import mybir

F32 = mybir.dt.float32
F16 = mybir.dt.float16
ALU = mybir.AluOpType
ACT = mybir.ActivationFunctionType
AX = mybir.AxisListType

P = 128
NB, T, D = 16, 112, 256
NT = NB * T
NH_S, NG, DH_S = 16, 4, 16
NJ = NH_S // NG
DPAD = 32
SC, CD = 375, 192
NKEY = NB * SC
NH, DH = 8, 128
INNER = NH * DH
FF = 4 * D
LN_EPS = 1e-5
WSCALE = 32.0

KT = 125
NKT = NKEY // KT
GT = 4
NGRP = NKT // GT
QB = 256
NQB = NT // QB
QT = QB // P
KC = 500
NKC = NKEY // KC
QC = 448
NQC = NT // QC
VW = 2 * DH + 1
KPAD = 16
SIM_SCALE = 1.5 * DH ** -0.5
LIFT = 5.545177444479562 / SIM_SCALE

WA_Q, WA_K, WA_V = 0, NJ * P, NJ * P + P
WA_N = WA_V + NG * DH_S

CH = 1000



def build(nc, xT, x, WA, Wo, ctxT, Wq, Wk, Wv, Wout, bout, W1T, b1, W2T, b2, o_dram, out):
    with ExitStack() as top:
        def sb(stack, name, shape, dt):
            return stack.enter_context(nc.sbuf_tensor(name, shape, dt))

        def sem(name):
            return top.enter_context(nc.semaphore(name))

        def credit(eng, s, n):
            eng.sem_inc(s, n)

        psum = top.enter_context(nc.psum_tensor("psum", [P, 8, 512], F32))

        res = sb(top, "res", [T, NB, D], F32)
        yT_hi = sb(top, "yT_hi", [P, 2, NT], F16)
        yT_lo = sb(top, "yT_lo", [P, 2, NT], F16)
        ident = sb(top, "ident", [P, P], F32)
        ones = sb(top, "ones", [P, P], F32)
        wout_hi = sb(top, "wout_hi", [P, NH, D], F16)
        wout_lo = sb(top, "wout_lo", [P, NH, D], F16)
        stats = sb(top, "stats", [T, NB, 6], F32)
        meanvar = sb(top, "meanvar", [T, NB, 2], F32)
        rstd = sb(top, "rstd", [T, NB], F32)
        norm_buf = [sb(top, f"norm_buf{r}", [T, D], F32) for r in range(2)]

        def counted(eng, start, end, step):
            return eng.Fori(start, end - step + 1, step)

        def chain(eng, s):
            n = [0]

            def run(ins):
                n[0] += 1
                ins.then_inc(s, 1)
                eng.wait_ge(s, n[0])
            return run

        def layer_norm(tag, to_dram=False):
            s_agg, s_sq, s_r = sem(tag + "agg"), sem(tag + "sqrt"), sem(tag + "rstd")
            s_n, s_t, s_hi, s_lo, s_cp = [sem(tag + n) for n in ("norm", "tr", "hi", "lo", "copy")]
            s_st = [sem(f"{tag}store{r}") for r in range(2)]
            with nc.Block() as block:

                @block.vector
                def _(v):
                    credit(v, s_lo, 2)
                    for b in range(NB):
                        v.bn_aggr(meanvar[:, b, :], stats[:, b, :]).then_inc(s_agg, 1)
                    v.wait_ge(s_agg, NB)
                    v.tensor_scalar(rstd[:, :], meanvar[:, :, 1], LN_EPS, None, ALU.add).then_inc(s_agg, 1)
                    v.wait_ge(s_sq, 1)
                    v.reciprocal(rstd[:, :], rstd[:, :]).then_inc(s_r, 1)
                    v.wait_ge(s_r, 1)

                    def low(b, r):
                        v.wait_ge(s_hi, b + r + 1)
                        v.tensor_tensor(yT_lo[:, :, bass.ds((b + r) * T, T)],
                                        psum[:, r, 0:2 * T].rearrange("p (k t) -> p k t", k=2),
                                        yT_hi[:, :, bass.ds((b + r) * T, T)],
                                        ALU.subtract).then_inc(s_lo, 1)

                    def normalise(b):
                        for r in range(2):
                            if to_dram:
                                v.wait_ge(s_st[r], b * 8 + 16)
                            else:
                                v.wait_ge(s_cp, b + r + 1)
                                v.wait_ge(s_t, b + r + 1)
                            v.tensor_scalar(norm_buf[r][:, :], res[:, b + r, :], meanvar[:, b + r, 0:1],
                                            rstd[:, bass.ds(b + r, 1)], ALU.subtract, ALU.mult).then_inc(s_n, 1)

                    if to_dram:
                        with counted(v, 0, NB, 2) as b:
                            normalise(b)
                    else:
                        normalise(0)
                        with counted(v, 0, NB - 2, 2) as b:
                            normalise(b + 2)
                            low(b, 0)
                            low(b, 1)
                        low(NB - 2, 0)
                        low(NB - 2, 1)

                @block.scalar
                def _(a):
                    a.wait_ge(s_agg, NB + 1)
                    a.activation(rstd[:, :], rstd[:, :], ACT.Sqrt).then_inc(s_sq, 1)
                    if not to_dram:
                        with counted(a, 0, NB, 2) as b:
                            for r in range(2):
                                a.wait_ge(s_t, b + r + 3)
                                a.activation(yT_hi[:, :, bass.ds((b + r) * T, T)],
                                             psum[:, r, 0:2 * T].rearrange("p (k t) -> p k t", k=2),
                                             ACT.Copy).then_inc(s_hi, 1)

                @block.gpsimd
                def _(g):
                    if to_dram:
                        return
                    credit(g, s_cp, 2)
                    with counted(g, 0, NB, 2) as b:
                        for r in range(2):
                            g.wait_ge(s_n, b + r + 1)
                            g.tensor_copy(res[:, b + r, :], norm_buf[r][:, :]).then_inc(s_cp, 1)

                @block.tensor
                def _(pe):
                    if to_dram:
                        return
                    credit(pe, s_t, 2)
                    with counted(pe, 0, NB, 2) as b:
                        for r in range(2):
                            pe.wait_ge(s_n, b + r + 1)
                            pe.wait_ge(s_lo, b + r + 1)
                            for k in range(2):
                                mm = pe.transpose(psum[:, r, k * T:(k + 1) * T],
                                                  norm_buf[r][:, k * P:(k + 1) * P], ident[0:T, 0:T])
                            mm.then_inc(s_t, 1)

                @block.sync
                def _(sp):
                    if not to_dram:
                        return
                    for r in range(2):
                        credit(sp, s_st[r], 16)
                    with counted(sp, 0, NB, 2) as b:
                        for r in range(2):
                            sp.wait_ge(s_n, b + r + 1)
                            sp.dma_start(out[bass.ds((b + r) * T, T), :], norm_buf[r][:, :]).then_inc(
                                s_st[r], 16)
                    for r in range(2):
                        sp.wait_ge(s_st[r], 16 + NB * 8)

        with ExitStack() as ab:
            ctx_hi = sb(ab, "ctx_hi", [P, NKEY + KPAD], F16)
            ctx_lo = sb(ab, "ctx_lo", [P, NKEY + KPAD], F16)
            ctx_s = sb(ab, "ctx_s", [P, NKEY + KPAD], F16)
            wq_hi = sb(ab, "wq_hi", [P, 2, INNER], F16)
            wq_lo = sb(ab, "wq_lo", [P, 2, INNER], F16)
            wkv = {n: [sb(ab, f"w{n}_{part}", [P, INNER], F16) for part in ("hi", "lo", "s_hi", "s_lo")]
                   for n in "kv"}

            with ExitStack() as pa:
                scratch = sb(pa, "scratch", [P, 6 * 8 * T], F32)
                x32 = scratch[:, 0:2 * NT].rearrange("p (k t) -> p k t", k=2)
                wa32 = scratch[:, 2 * NT:2 * NT + 2 * WA_N].rearrange("p (k n) -> p k n", k=2)
                tiles = [scratch[0:T, i * 8 * T:(i + 1) * 8 * T].rearrange("p (h t) -> p h t", h=8)
                         for i in range(6)]
                shifted, prob, probT = tiles[0:2], tiles[2:4], tiles[4:6]
                wa_hi = sb(pa, "wa_hi", [P, 2, WA_N], F16)
                wa_lo = sb(pa, "wa_lo", [P, 2, WA_N], F16)
                wo32 = sb(pa, "wo32", [P, 2, D], F32)
                q_hi = sb(pa, "q_hi", [P, NJ, NT], F16)
                q_lo = sb(pa, "q_lo", [P, NJ, NT], F16)
                kb_hi = sb(pa, "kb_hi", [P, NG, NT], F16)
                kb_lo = sb(pa, "kb_lo", [P, NG, NT], F16)
                vs = sb(pa, "vs", [T, NB, NG, DH_S + 1], F32)
                stage = [sb(pa, f"stage{r}", [P, 2, INNER], F32) for r in range(2)]
                mx = [sb(pa, f"mx{r}", [T, 8], F32) for r in range(2)]
                rden = sb(pa, "rden", [T, 8], F32)
                att = sb(pa, "att", [T, D], F32)
                attT = sb(pa, "attT", [P, 2, T], F32)

                s_x, s_wa, s_wo, s_res = sem("a_x"), sem("a_wa"), sem("a_wo"), sem("a_res")
                s_stage = [sem(f"a_stage{r}") for r in range(2)]
                s_staged = sem("a_staged")
                s_const, s_g, s_prep, s_split = sem("a_const"), sem("a_g"), sem("a_prep"), sem("a_split")
                s_pj, s_ph, s_pl = sem("a_pj"), sem("a_ph"), sem("a_pl")
                (s_s, s_mx, s_sub, s_exp, s_T, s_ptc, s_av, s_rd, s_nrm, s_at, s_atc, s_wop, s_add, s_bn) = [
                    sem("a_" + n) for n in ("s", "mx", "sub", "exp", "T", "ptc", "av", "rd", "nrm", "at",
                                            "atc", "wop", "add", "bn")]

                def halves(n, src):
                    return [(lambda st: st[:, 0, 0:n], src[0:P]), (lambda st: st[0:64, 1, 0:n], src[P:CD]),
                            (lambda st: st[64:P, 1, 0:n], src[P:CD])]

                tasks = [[(lambda st: st[:, :, 0:INNER], Wq.rearrange("(k p) n -> p k n", p=P))],
                         halves(INNER, Wk), halves(INNER, Wv),
                         [(lambda st: st[:, :, :].rearrange("p a b -> p (a b)")[:, 0:NH * D].rearrange(
                             "p (h n) -> p h n", h=NH), Wout.rearrange("(h d) n -> d h n", d=DH))]]
                tasks += [halves(CH, ctxT[:, c * CH:(c + 1) * CH]) for c in range(NKEY // CH)]

                with nc.Block() as block:

                    @block.sync
                    def _(sp):
                        sp.dma_start(x32[:, :, :], xT.rearrange("(k p) t -> p k t", p=P)).then_inc(s_x, 16)
                        sp.dma_start(wa32[:, :, :], WA.rearrange("(k p) n -> p k n", p=P)).then_inc(s_wa, 16)
                        sp.dma_start(wo32[:, :, :], Wo.rearrange("(k p) n -> p k n", p=P)).then_inc(s_wo, 16)
                        sp.dma_start(res[:, :, :], x.rearrange("(b t) d -> t b d", t=T)).then_inc(s_res, 16)
                        for i, task in enumerate(tasks):
                            if i >= 2:
                                sp.wait_ge(s_staged, i - 1)
                            for dst, src in task:
                                sp.dma_start(dst(stage[i % 2]), src).then_inc(s_stage[i % 2], 16)

                    @block.gpsimd
                    def _(g):
                        run = chain(g, s_g)
                        run(g.memset(ident[:, :], 0.0))
                        g.affine_select(out=ident[:, :], in_=ident[:, :], compare_op=ALU.not_equal, fill=1.0,
                                        base=0, pattern=[[-1, P]], channel_multiplier=1).then_inc(s_const, 1)
                        g.memset(ones[:, :], 1.0).then_inc(s_const, 1)
                        for t in (ctx_hi, ctx_lo, ctx_s):
                            run(g.memset(t[:, NKEY:NKEY + KPAD], 0.0))
                        for n in "kv":
                            run(g.memset(wkv[n][3][64:P, :], 0.0))
                        loaded = [0, 0]
                        for i, task in enumerate(tasks):
                            st = stage[i % 2]
                            loaded[i % 2] += 16 * len(task)
                            g.wait_ge(s_stage[i % 2], loaded[i % 2])
                            if i < 4:
                                flat = st[:, :, :].rearrange("p a b -> p (a b)")[:, 0:NH * D] if i == 3 \
                                    else st[:, :, 0:INNER]
                                run(g.tensor_scalar(flat, flat, WSCALE, 1.0, ALU.mult, ALU.mult))
                            if i == 0:
                                run(g.tensor_copy(wq_hi[:, :, :], flat))
                                run(g.tensor_tensor(wq_lo[:, :, :], flat, wq_hi[:, :, :], ALU.subtract))
                            elif i in (1, 2):
                                hi, lo, s_hi, s_lo = wkv["kv"[i - 1]]
                                run(g.tensor_copy(hi[:, :], st[:, 0, 0:INNER]))
                                run(g.tensor_tensor(lo[:, :], st[:, 0, 0:INNER], hi[:, :], ALU.subtract))
                                run(g.tensor_copy(s_hi[:, :], st[:, 1, 0:INNER]))
                                run(g.tensor_tensor(s_lo[0:64, :], st[0:64, 1, 0:INNER], s_hi[0:64, :],
                                                    ALU.subtract))
                            elif i == 3:
                                hi, lo = [w[:, :, :].rearrange("p h n -> p (h n)") for w in (wout_hi, wout_lo)]
                                run(g.tensor_copy(hi, flat))
                                run(g.tensor_tensor(lo, flat, hi, ALU.subtract))
                            else:
                                c0 = (i - 4) * CH
                                hi, lo, s = [t[:, c0:c0 + CH] for t in (ctx_hi, ctx_lo, ctx_s)]
                                run(g.tensor_copy(hi, st[:, 0, 0:CH]))
                                run(g.tensor_tensor(lo, st[:, 0, 0:CH], hi, ALU.subtract))
                                run(g.tensor_copy(s, st[:, 1, 0:CH]))
                                s_low = ctx_s[64:P, c0:c0 + CH]
                                run(g.tensor_tensor(s_low, st[64:P, 1, 0:CH], s_low, ALU.subtract))
                            g.sem_inc(s_staged, 1)

                    @block.tensor
                    def _(pe):
                        pe.wait_ge(s_split, 4)
                        with pe.Fori(0, NQC) as c:
                            cols = bass.ds(c * QC, QC)
                            for j in range(NJ + 1):
                                pe.wait_ge(s_pl, c * 9 + (j + 1 if j < NJ else 8))
                                w = slice(WA_Q + j * P, WA_Q + (j + 1) * P)
                                for n, (k, wt, xt) in enumerate([(k, wt, xt) for k in range(2) for wt, xt in (
                                        (wa_hi, yT_hi), (wa_hi, yT_lo), (wa_lo, yT_hi))]):
                                    mm = pe.matmul(psum[:, j, 0:QC], lhsT=wt[:, k, w], rhs=xt[:, k, cols],
                                                   start=(n == 0), stop=(n == 5))
                                mm.then_inc(s_pj, 1)
                            pe.wait_ge(s_pl, c * 9 + 9)
                            for i in range(QC // T):
                                for n, (k, wt, xt) in enumerate([(k, wt, xt) for k in range(2) for wt, xt in (
                                        (wa_hi, yT_hi), (wa_hi, yT_lo), (wa_lo, yT_hi))]):
                                    mm = pe.matmul(psum[0:T, 5, i * 64:(i + 1) * 64],
                                                   lhsT=xt[:, k, bass.ds(c * QC + i * T, T)],
                                                   rhs=wt[:, k, WA_V:WA_N], start=(n == 0), stop=(n == 5))
                            mm.then_inc(s_pj, 1)

                        pe.wait_ge(s_pl, 9 + 9 * NQC)
                        pe.wait_ge(s_const, 2)
                        pe.wait_ge(s_wo, 16)

                        def scores(b, r):
                            u = b * 2 + r
                            pe.wait_ge(s_sub, u + 1)
                            tok = bass.ds(b * T, T)
                            for jj in range(2):
                                j = 2 * r + jj
                                for n, (q, k) in enumerate(((q_hi, kb_hi), (q_hi, kb_lo), (q_lo, kb_hi))):
                                    mm = pe.matmul(psum[0:T, j, 0:NG * T].rearrange("p (g t) -> p g t", g=NG),
                                                   lhsT=q[:, j, tok], rhs=k[:, :, tok],
                                                   start=(n == 0), stop=(n == 2))
                            mm.then_inc(s_s, 1)

                        def transposes(b, r):
                            u = b * 2 + r
                            pe.wait_ge(s_exp, u + 3)
                            pe.wait_ge(s_ptc, u + 1)
                            for hh in range(8):
                                mm = pe.transpose(psum[0:T, 4 + hh // 4, (hh % 4) * T:(hh % 4 + 1) * T],
                                                  prob[r][:, hh, :], ident[0:T, 0:T])
                            mm.then_inc(s_T, 1)

                        def weighted_v(b, r):
                            u = b * 2 + r
                            pe.wait_ge(s_ptc, u + 2)
                            pe.wait_ge(s_nrm, u + 1)
                            for hh in range(8):
                                mm = pe.matmul(psum[0:T, 6, hh * (DH_S + 1):(hh + 1) * (DH_S + 1)],
                                               lhsT=probT[r][:, hh, :], rhs=vs[:, b, hh % NG, :],
                                               start=True, stop=True)
                            mm.then_inc(s_av, 1)

                        def att_transposes(b):
                            pe.wait_ge(s_nrm, b * 2 + 3)
                            pe.wait_ge(s_add, b + 1)
                            for k in range(2):
                                mm = pe.transpose(psum[:, 7, k * T:(k + 1) * T], att[:, k * P:(k + 1) * P],
                                                  ident[0:T, 0:T])
                            mm.then_inc(s_at, 1)

                        def project(b):
                            pe.wait_ge(s_atc, b + 1)
                            for k in range(2):
                                mm = pe.matmul(psum[0:T, 7, D:2 * D], lhsT=attT[:, k, :], rhs=wo32[:, k, :],
                                               start=(k == 0), stop=(k == 1))
                            mm.then_inc(s_wop, 1)

                        def batch(b, first=False, last=False):
                            for r in range(2):
                                transposes(b, r)
                                if r == 0 and not first:
                                    att_transposes(b - 1)
                                if not last:
                                    scores(b + 1, r)
                                weighted_v(b, r)
                                if r == 0 and not first:
                                    project(b - 1)

                        credit(pe, s_T, 2)
                        credit(pe, s_av, 2)
                        credit(pe, s_at, 1)
                        scores(0, 0)
                        scores(0, 1)
                        batch(0, first=True)
                        with pe.Fori(1, NB - 1) as b:
                            batch(b)
                        batch(NB - 1, last=True)
                        att_transposes(NB - 1)
                        project(NB - 1)

                    @block.scalar
                    def _(a):
                        with a.Fori(0, NQC) as c:
                            cols = bass.ds(c * QC, QC)
                            for j in range(NJ):
                                a.wait_ge(s_pj, c * 6 + j + 1)
                                a.activation(q_hi[:, j, cols], psum[:, j, 0:QC], ACT.Copy,
                                             scale=1 / WSCALE).then_inc(s_ph, 1)
                            a.wait_ge(s_pj, c * 6 + NJ + 1)
                            a.wait_ge(s_prep, 2)
                            for g in range(NG):
                                rows32 = slice(g * DPAD, (g + 1) * DPAD)
                                a.activation(kb_hi[rows32, g, cols], psum[rows32, NJ, 0:QC], ACT.Copy,
                                             scale=1 / WSCALE).then_inc(s_ph, 1)

                        def exps(b, r):
                            u = b * 2 + r
                            a.wait_ge(s_sub, u + 3)
                            a.wait_ge(s_T, u + 1)
                            a.activation(prob[r][:, :, :], shifted[r][:, :, :], ACT.Exp,
                                         scale=DH_S ** -0.5).then_inc(s_exp, 1)

                        def copy_probT(b, r):
                            u = b * 2 + r
                            a.wait_ge(s_T, u + 3)
                            a.wait_ge(s_av, u + 1)
                            a.activation(probT[r][:, :, :].rearrange("p (c h) t -> p c (h t)", c=2),
                                         psum[0:T, 4:6, 0:4 * T], ACT.Copy).then_inc(s_ptc, 1)

                        def copy_attT(b):
                            a.wait_ge(s_at, b + 2)
                            a.activation(attT[:, :, :], psum[:, 7, 0:2 * T].rearrange("p (k t) -> p k t", k=2),
                                         ACT.Copy).then_inc(s_atc, 1)

                        def batch(b, first=False, last=False):
                            exps(b, 1)
                            copy_probT(b, 0)
                            if not first:
                                copy_attT(b - 1)
                            if not last:
                                exps(b + 1, 0)
                            copy_probT(b, 1)

                        credit(a, s_ptc, 1)
                        credit(a, s_exp, 2)
                        exps(0, 0)
                        batch(0, first=True)
                        with a.Fori(1, NB - 1) as b:
                            batch(b)
                        batch(NB - 1, last=True)
                        copy_attT(NB - 1)

                    @block.vector
                    def _(v):
                        v.memset(kb_hi[:, :, :].bitcast(F32), 0.0).then_inc(s_prep, 1)
                        v.memset(kb_lo[:, :, :].bitcast(F32), 0.0).then_inc(s_prep, 1)
                        v.memset(vs[:, :, :, :], 1.0).then_inc(s_prep, 1)
                        v.wait_ge(s_x, 16)
                        v.tensor_copy(yT_hi[:, :, :], x32[:, :, :]).then_inc(s_split, 1)
                        v.wait_ge(s_wa, 16)
                        v.tensor_scalar(wa_hi[:, :, :], wa32[:, :, :], WSCALE, None, ALU.mult).then_inc(s_split, 1)
                        v.wait_ge(s_split, 2)
                        v.tensor_tensor(yT_lo[:, :, :], x32[:, :, :], yT_hi[:, :, :],
                                        ALU.subtract).then_inc(s_split, 1)
                        v.scalar_tensor_tensor(wa_lo[:, :, :], wa32[:, :, :], WSCALE, wa_hi[:, :, :],
                                               ALU.mult, ALU.subtract).then_inc(s_split, 1)
                        credit(v, s_pl, 9)
                        v.wait_ge(s_prep, 3)
                        with v.Fori(0, NQC) as c:
                            cols = bass.ds(c * QC, QC)
                            for j in range(NJ):
                                v.wait_ge(s_ph, c * 8 + j + 1)
                                v.scalar_tensor_tensor(q_lo[:, j, cols], psum[:, j, 0:QC], 1 / WSCALE,
                                                       q_hi[:, j, cols], ALU.mult, ALU.subtract).then_inc(s_pl, 1)
                            for g in range(NG):
                                rows32 = slice(g * DPAD, (g + 1) * DPAD)
                                v.wait_ge(s_ph, c * 8 + NJ + g + 1)
                                v.scalar_tensor_tensor(kb_lo[rows32, g, cols], psum[rows32, NJ, 0:QC], 1 / WSCALE,
                                                       kb_hi[rows32, g, cols], ALU.mult,
                                                       ALU.subtract).then_inc(s_pl, 1)
                            v.wait_ge(s_pj, c * 6 + 6)
                            v.tensor_scalar(vs[:, bass.ds(c * 4, 4), :, 0:DH_S],
                                            psum[0:T, 5, 0:256].rearrange("p (b g d) -> p b g d", b=4, g=NG),
                                            1 / WSCALE, None, ALU.mult).then_inc(s_pl, 1)

                        def shift(b, r):
                            u = b * 2 + r
                            sc = psum[0:T, 2 * r:2 * r + 2, 0:4 * T].rearrange("p c (h t) -> p c h t", h=4)
                            v.wait_ge(s_s, u + 1)
                            v.wait_ge(s_exp, u + 1)
                            v.tensor_reduce(mx[r][:, :].rearrange("p (c h) -> p c h", c=2), sc, AX.X,
                                            ALU.max).then_inc(s_mx, 1)
                            v.wait_ge(s_mx, u + 1)
                            for c in range(2):
                                ins = v.tensor_tensor(
                                    shifted[r][:, 4 * c:4 * c + 4, :],
                                    psum[0:T, 2 * r + c, 0:4 * T].rearrange("p (h t) -> p h t", h=4),
                                    mx[r][:, 4 * c:4 * c + 4].unsqueeze(2).broadcast_to([T, 4, T]), ALU.subtract)
                            ins.then_inc(s_sub, 1)

                        def normalise(b, r):
                            u = b * 2 + r
                            av = psum[0:T, 6, 0:8 * (DH_S + 1)].rearrange("p (h w) -> p h w", h=8)
                            v.wait_ge(s_av, u + 3)
                            v.reciprocal(rden[:, :], av[:, :, DH_S]).then_inc(s_rd, 1)
                            v.wait_ge(s_at, b + 1)
                            v.wait_ge(s_rd, u + 1)
                            heads = att[:, :].rearrange("p (g j d) -> p j g d", g=NG, j=NJ)
                            for jj in range(2):
                                ins = v.tensor_tensor(
                                    heads[:, 2 * r + jj, :, :], av[:, 4 * jj:4 * jj + 4, 0:DH_S],
                                    rden[:, 4 * jj:4 * jj + 4].unsqueeze(2).broadcast_to([T, 4, DH_S]), ALU.mult)
                            ins.then_inc(s_nrm, 1)

                        def residual(b):
                            v.wait_ge(s_wop, b + 1)
                            v.tensor_tensor(res[:, b, :], psum[0:T, 7, D:2 * D], res[:, b, :],
                                            ALU.add).then_inc(s_add, 1)
                            v.wait_ge(s_add, b + 2)
                            v.bn_stats(stats[:, b, :], res[:, b, :]).then_inc(s_bn, 1)

                        def batch(b, first=False, last=False):
                            shift(b, 1)
                            normalise(b, 0)
                            if not first:
                                residual(b - 1)
                            if not last:
                                shift(b + 1, 0)
                            normalise(b, 1)

                        credit(v, s_sub, 2)
                        credit(v, s_nrm, 1)
                        credit(v, s_add, 1)
                        v.wait_ge(s_res, 16)
                        shift(0, 0)
                        batch(0, first=True)
                        with v.Fori(1, NB - 1) as b:
                            batch(b)
                        batch(NB - 1, last=True)
                        residual(NB - 1)

            layer_norm("ln1_")

            with ExitStack() as pb:
                k_hi = sb(pb, "k_hi", [P, 2, NKEY + KPAD], F16)
                k_lo = sb(pb, "k_lo", [P, 2, NKEY + KPAD], F16)
                v_all = sb(pb, "v_all", [P, NKT, VW], F16)
                q_hi = sb(pb, "qx_hi", [P, 2, QB], F16)
                q_lo = sb(pb, "qx_lo", [P, 2, QB], F16)
                shifted = [sb(pb, f"sx{r}", [P, GT, QB], F32) for r in range(2)]
                e32 = [sb(pb, f"e32_{r}", [P, GT, QB], F32) for r in range(2)]
                e_hi = [sb(pb, f"e_hi{r}", [P, GT, QB], F16) for r in range(2)]
                e_lo = [sb(pb, f"e_lo{r}", [P, GT, QB], F16) for r in range(2)]
                part_max = sb(pb, "part_max", [P, QT, NKC], F32)
                row_max = sb(pb, "row_max", [P, QT], F32)
                diag = sb(pb, "diag", [P, QB], F32)
                max_b = sb(pb, "max_b", [P, QB], F32)
                o_buf = sb(pb, "o_buf", [P, QT, VW], F32)

                (s_init, s_part, s_qk, s_sub, s_e, s_hi, s_lo, s_av, s_oev, s_od, s_rm, s_dg) = [
                    sem("b_" + n) for n in ("init", "part", "qk", "sub", "e", "hi", "lo", "av", "oev",
                                            "od", "rm", "dg")]
                s_full = [sem(f"b_full{i}") for i in range(2)]
                s_free = [sem(f"b_free{i}") for i in range(2)]
                HG = NQB * NGRP
                LAST_QB = NQB - 1

                START, START_PARTS = (26, 24), 1 + NKC + NGRP
                MID, MID_PARTS = (15, 13), 3
                ENDING, ENDING_PARTS = (20, 18), 1 + NGRP
                MID7 = (14, 12)
                HEAD = [LAST_QB * MID[i] + ENDING[i] for i in range(2)]
                HEAD_PARTS = LAST_QB * MID_PARTS + ENDING_PARTS

                class Turns:

                    def __init__(self, banks=(0, 0), parts=0):
                        self.banks, self.parts = list(banks), parts
                        self.more, self.more_parts = [0, 0], 0

                    def bank(self, i):
                        self.more[i] += 1
                        return self.banks[i] + self.more[i]

                    def part(self):
                        self.more_parts += 1
                        return self.parts + self.more_parts

                    def counts(self):
                        return self.banks, self.parts, list(self.more), self.more_parts

                    def rewind(self, counts):
                        self.banks, self.parts, self.more, self.more_parts = counts

                    def skip(self, banks, parts):
                        self.banks = [self.banks[i] + banks[i] for i in range(2)]
                        self.parts = self.parts + parts

                def block_turns(h, qb, kind):
                    mid, parts = (MID, MID_PARTS) if kind in ("k", "v") else (MID7, 1)
                    return Turns([START[i] + h * HEAD[i] + qb * mid[i] for i in range(2)],
                                 START_PARTS + h * HEAD_PARTS + qb * parts)

                def walk(eng, turns, kind, step):
                    def m(bank, piece):
                        return [("m", bank, piece)]

                    def v(bank, tile_group):
                        return [("v", bank, tile_group)] if kind == "v" else []

                    q, spread = [("q", 0, 0)], [("b", 0, 0)]
                    if kind == "v":
                        early = [(q, [], v(1, 0)), (m(0, 0), m(1, 0), v(0, 1)),
                                 (m(1, 1), m(0, 1), v(1, 2)), (m(0, 2), m(1, 2), v(0, 3))]
                    elif kind == "k":
                        early = [(q, [("k", 1, 0)], []), ([("k", 0, 1)], m(1, 0), m(0, 0)),
                                 (m(1, 1), m(0, 1), []), (m(1, 2), m(0, 2), [])]
                    else:
                        early = [(q, [], []), ([], m(0, 0), m(1, 0)),
                                 (m(0, 1), m(1, 1), []), (m(0, 2), m(1, 2), [])]
                    for s in range(4):
                        step(s, s % 2, *(early[s] if kind else ([], [], [])))
                    trips = 3
                    per = [0, 0] if not kind else [4, 4] if kind == "v" else [3, 3]
                    per_parts = 2 if kind == "v" else 0
                    with eng.Fori(0, trips) as j:
                        saved = turns.counts()
                        turns.skip([j * n for n in per], j * per_parts)
                        s, p = j * 2 + 4, j * 3 + 3
                        if kind == "v":
                            step(s, 0, m(1, p), m(0, p), m(1, p + 1) + v(0, s))
                            step(s + 1, 1, m(1, p + 2), m(0, p + 1), v(1, s + 1) + m(0, p + 2))
                        elif kind:
                            step(s, 0, m(1, p), m(0, p), m(1, p + 1))
                            step(s + 1, 1, m(0, p + 1), m(1, p + 2), m(0, p + 2))
                        else:
                            step(s, 0, [], [], [])
                            step(s + 1, 1, [], [], [])
                        turns.rewind(saved)
                    turns.skip([trips * n for n in per], trips * per_parts)
                    step(10, 0, [], spread if kind else [], v(1, 10))
                    step(11, 1, [], [], v(0, 11))

                def heads(eng, block_steps):
                    with eng.Fori(0, NH - 1) as h:
                        with eng.Fori(0, LAST_QB) as qb:
                            block_steps(h, qb, "k")
                        block_steps(h, LAST_QB, "v")
                    with eng.Fori(0, LAST_QB) as qb:
                        block_steps(NH - 1, qb, "m")
                    block_steps(NH - 1, LAST_QB, "")

                def start_tasks(eng, side):
                    t = Turns()
                    side(t, ("q", 0, 0), 0, 0, 0, 0)
                    with counted(eng, 0, NKC, 2) as c:
                        loop = Turns([1 + c // 2, c // 2], 1 + c)
                        for r in range(2):
                            side(loop, ("k", 1 - r, r), 0, 0, c, 0)
                    with counted(eng, 0, NGRP, 2) as c:
                        loop = Turns([7 + c // 2 * 3, 6 + c // 2 * 3], 1 + NKC + c)
                        for r in range(2):
                            for task in (("m", 0, c + r), ("m", 1, c + r), ("v", r, c + r)):
                                side(loop, task, 0, 0, 0, 0)
                    t = Turns([START[0] - 1, START[1]], START_PARTS)
                    side(t, ("b", 0, 0), 0, 0, 0, 0)


                with nc.Block() as block:

                    @block.tensor
                    def _(pe):
                        def scores(f, step, hp, np_, r):
                            pe.wait_ge(s_sub, f + 1)
                            for i in range(GT):
                                keys = bass.ds((step * GT + i) * KT, P)
                                for n, (k, q) in enumerate(((k_hi, q_hi), (k_hi, q_lo), (k_lo, q_hi))):
                                    mm = pe.matmul(psum[:, 2 * r + i // 2, (i % 2) * QB:(i % 2 + 1) * QB],
                                                   lhsT=k[:, hp, keys], rhs=q[:, np_, :],
                                                   start=(n == 0), stop=(n == 2))
                            mm.then_inc(s_qk, 1)

                        def attend(f, step, r, first=False, last=False):
                            pe.wait_ge(s_lo, f + 3)
                            for i in range(GT):
                                for t in range(QT):
                                    start, stop = first and i == 0, last and i == GT - 1
                                    hi, lo = (e_hi, VW), (e_lo, DH + 1)
                                    for n, (e, w) in enumerate((lo, hi) if stop else (hi, lo)):
                                        mm = pe.matmul(psum[:, 4 + t, 0:w], lhsT=e[r][0:KT, i, t * P:(t + 1) * P],
                                                       rhs=v_all[0:KT, step * GT + i, 0:w],
                                                       start=start and n == 0, stop=stop and n == 1)
                            mm.then_inc(s_av, 1)

                        def side(turns, task, h, n, k0, q0):
                            what, i, index = task
                            pe.wait_ge(s_free[i], turns.bank(i))
                            hd = bass.ds(h * DH, DH)
                            bank = psum[:, 6 + i, :]
                            if what == "q":
                                for x, (k, w, y) in enumerate([(k, w, y) for k in range(2) for w, y in (
                                        (wq_hi, yT_hi), (wq_hi, yT_lo), (wq_lo, yT_hi))]):
                                    mm = pe.matmul(bank[:, 0:QB], lhsT=w[:, k, hd], rhs=y[:, k, bass.ds(q0, QB)],
                                                   start=(x == 0), stop=(x == 5))
                            elif what == "k":
                                whi, wlo, wshi, wslo = wkv["k"]
                                for x, (w, y) in enumerate(((whi, ctx_hi), (whi, ctx_lo), (wlo, ctx_hi),
                                                            (wshi, ctx_s), (wslo, ctx_s))):
                                    mm = pe.matmul(bank[:, 0:KC], lhsT=w[:, hd],
                                                   rhs=y[:, bass.ds((k0 + index) * KC, KC)],
                                                   start=(x == 0), stop=(x == 4))
                            elif what == "v":
                                whi, wlo, wshi, wslo = wkv["v"]
                                for g in range(GT):
                                    keys = bass.ds((index * GT + g) * KT, P)
                                    for x, (y, w) in enumerate(((ctx_hi, whi), (ctx_hi, wlo), (ctx_lo, whi),
                                                                (ctx_s, wshi), (ctx_s, wslo))):
                                        mm = pe.matmul(bank[:, g * DH:(g + 1) * DH], lhsT=y[:, keys],
                                                       rhs=w[:, hd], start=(x == 0), stop=(x == 4))
                            elif what == "m":
                                mm = pe.matmul(bank[:, 0:KC], lhsT=q_hi[:, n & 1, i * P:(i + 1) * P],
                                               rhs=k_hi[:, h & 1, bass.ds(index * KC, KC)], start=True, stop=True)
                            else:
                                pe.wait_ge(s_dg, n + 1)
                                mm = pe.matmul(bank[:, 0:QB], lhsT=ones[:, :], rhs=diag[:, :],
                                               start=True, stop=True)
                            mm.then_inc(s_full[i], 1)

                        def block_steps(h, qb, kind):
                            n = h * NQB + qb
                            f0 = n * NGRP
                            turns = block_turns(h, qb, kind)
                            h1, q1 = (h + 1, 0) if kind == "v" else (h, qb * QB + QB)

                            def sides(tasks):
                                for task in tasks:
                                    side(turns, task, h + 1 if task[0] == "k" else h1, n + 1, qb * 2, q1)

                            def step(s, r, before, between, after):
                                sides(before)
                                if isinstance(s, int) and s >= NGRP - 2:
                                    if kind:
                                        scores(f0 + s + 2, s + 2 - NGRP, h1 & 1, (n + 1) & 1, r)
                                else:
                                    scores(f0 + s + 2, s + 2, h & 1, n & 1, r)
                                sides(between)
                                first = isinstance(s, int) and s == 0
                                if first:
                                    pe.wait_ge(s_oev, n + 1)
                                attend(f0 + s, s, r, first, isinstance(s, int) and s == NGRP - 1)
                                sides(after)

                            walk(pe, turns, kind, step)

                        credit(pe, s_av, 2)
                        pe.wait_ge(s_init, 4)
                        start_tasks(pe, side)
                        for i in range(2):
                            pe.wait_ge(s_free[i], START[i] + (1 if i else 0))
                        scores(0, 0, 0, 0, 0)
                        scores(1, 1, 0, 0, 1)
                        heads(pe, block_steps)

                    @block.scalar
                    def _(a):
                        def exps(f, r):
                            a.wait_ge(s_sub, f + 3)
                            a.wait_ge(s_lo, f + 1)
                            a.activation(e32[r][0:KT, :, :], shifted[r][0:KT, :, :], ACT.Exp,
                                         scale=SIM_SCALE).then_inc(s_e, 1)
                            a.wait_ge(s_av, f + 1)
                            a.activation(e_hi[r][0:KT, :, :], shifted[r][0:KT, :, :], ACT.Exp,
                                         scale=SIM_SCALE).then_inc(s_hi, 1)

                        def block_steps(n, groups):
                            with counted(a, 2, groups, 2) as s:
                                for r in range(2):
                                    exps(n * NGRP + s + r, r)
                            a.wait_ge(s_av, n * NGRP + NGRP + 2)
                            a.wait_ge(s_od, n * 16 + 16)
                            a.activation(o_buf[:, :, :], psum[:, 4:6, 0:VW], ACT.Copy).then_inc(s_oev, 1)

                        credit(a, s_hi, 2)
                        credit(a, s_oev, 1)
                        exps(0, 0)
                        exps(1, 1)
                        with a.Fori(0, NH * NQB - 1) as n:
                            block_steps(n, NGRP + 2)
                        block_steps(NH * NQB - 1, NGRP)

                    @block.vector
                    def _(v):
                        def shift(f, r):
                            v.wait_ge(s_qk, f + 1)
                            v.wait_ge(s_hi, f + 1)
                            for c in range(2):
                                ins = v.tensor_tensor(
                                    shifted[r][0:KT, 2 * c:2 * c + 2, :],
                                    psum[0:KT, 2 * r + c, :].rearrange("p (i q) -> p i q", i=2),
                                    max_b[0:KT, :].unsqueeze(1).broadcast_to([KT, 2, QB]), ALU.subtract)
                            ins.then_inc(s_sub, 1)

                        def split(turns, dst_hi, dst_lo, src):
                            v.tensor_scalar(dst_hi, src, 1 / WSCALE, None, ALU.mult).then_inc(s_part, 1)
                            v.wait_ge(s_part, turns.part())
                            return v.scalar_tensor_tensor(dst_lo, src, 1 / WSCALE, dst_hi, ALU.mult, ALU.subtract)

                        def side(turns, task, h, n, k0, q0):
                            what, i, index = task
                            number = turns.bank(i)
                            bank = psum[:, 6 + i, :]
                            if what in "qkv":
                                v.wait_ge(s_full[i], number)
                            if what == "q":
                                ins = split(turns, q_hi[:, n & 1, :], q_lo[:, n & 1, :], bank[:, 0:QB])
                            elif what == "k":
                                cols = bass.ds((k0 + index) * KC, KC)
                                ins = split(turns, k_hi[:, h & 1, cols], k_lo[:, h & 1, cols], bank[:, 0:KC])
                            elif what == "v":
                                tiles4 = bass.ds(index * GT, GT)
                                ins = split(turns, v_all[0:KT, tiles4, 0:DH], v_all[0:KT, tiles4, DH + 1:VW],
                                            psum[0:KT, 6 + i, :].rearrange("p (g d) -> p g d", g=GT))
                            elif what == "m":
                                v.wait_ge(s_full[i], number)
                                one = slice(index, index + 1) if isinstance(index, int) else bass.ds(index, 1)
                                ins = v.tensor_reduce(part_max[:, i, one], bank[:, 0:KC], AX.X, ALU.max)
                            else:
                                v.wait_ge(s_free[0], number)
                                v.wait_ge(s_free[1], turns.banks[1] + turns.more[1] + 1)
                                v.tensor_reduce(row_max[:, :], part_max[:, :, :], AX.X, ALU.max).then_inc(s_rm, 1)
                                v.wait_ge(s_rm, n + 1)
                                v.tensor_tensor(diag[:, :].rearrange("p (t q) -> p t q", t=QT),
                                                ident[:, :].unsqueeze(1).broadcast_to([P, QT, P]),
                                                row_max[:, :].unsqueeze(2).broadcast_to([P, QT, P]),
                                                ALU.mult).then_inc(s_dg, 1)
                                v.wait_ge(s_full[i], number)
                                ins = v.tensor_scalar(max_b[:, :], bank[:, 0:QB], -LIFT, None, ALU.add)
                            ins.then_inc(s_free[i], 1)
                            if what == "b":
                                v.wait_ge(s_free[i], number + 1)

                        def block_steps(h, qb, kind):
                            n = h * NQB + qb
                            f0 = n * NGRP
                            turns = block_turns(h, qb, kind)
                            h1 = h + 1 if kind == "v" else h

                            def sides(tasks):
                                for task in tasks:
                                    side(turns, task, h + 1 if task[0] == "k" else h1, n + 1, qb * 2, 0)

                            def step(s, r, before, between, after):
                                sides(before)
                                spread = [t for t in between if t[0] == "b"]
                                sides(spread)
                                if kind or not (isinstance(s, int) and s >= NGRP - 2):
                                    shift(f0 + s + 2, r)
                                sides([t for t in between if t[0] != "b"])
                                sides(after)

                            walk(v, turns, kind, step)

                        credit(v, s_sub, 2)
                        for i in range(2):
                            credit(v, s_free[i], 1)
                        for t in (k_hi, k_lo):
                            v.memset(t[:, :, NKEY:NKEY + KPAD], 0.0).then_inc(s_init, 1)
                        v.memset(v_all[:, :, DH:DH + 1], 1.0).then_inc(s_init, 1)
                        v.memset(part_max[:, :, :], 0.0).then_inc(s_init, 1)
                        v.wait_ge(s_init, 4)
                        start_tasks(v, side)
                        shift(0, 0)
                        shift(1, 1)
                        heads(v, block_steps)

                    @block.gpsimd
                    def _(g):
                        credit(g, s_lo, 2)
                        with counted(g, 0, NH * HG, 2) as f:
                            for r in range(2):
                                g.wait_ge(s_hi, f + (r + 3))
                                g.tensor_tensor(e_lo[r][0:KT, :, :], e32[r][0:KT, :, :], e_hi[r][0:KT, :, :],
                                                ALU.subtract).then_inc(s_lo, 1)

                    @block.sync
                    def _(sp):
                        credit(sp, s_od, 16)
                        with sp.Fori(0, NH) as h:
                            with sp.Fori(0, NQB) as qb:
                                sp.wait_ge(s_oev, h * NQB + qb + 2)
                                sp.dma_start(o_dram[bass.ds(qb * QB, QB), bass.ds(h * VW, VW)].rearrange(
                                    "(t p) w -> p t w", p=P), o_buf[:, :, :]).then_inc(s_od, 16)
                        sp.wait_ge(s_od, NH * NQB * 16 + 16)

        with ExitStack() as cd:
            w1t = sb(cd, "w1t", [P, 2, FF], F16)
            w2t = sb(cd, "w2t", [P, FF // P, D], F16)
            b1s = sb(cd, "b1s", [P, FF // P], F32)
            bout_b = sb(cd, "bout_b", [T, D], F32)
            b2_b = sb(cd, "b2_b", [T, D], F32)

            with ExitStack() as pc:
                w32 = [sb(pc, f"w32_{i}", [P, 2 * FF], F32) for i in range(2)]
                below = [sb(pc, f"below{i}", [P, 2 * FF], F32) for i in range(2)]
                scale, above_of, below_of = [sb(pc, n, [P, 2], F32) for n in ("scale", "above_of", "below_of")]
                sum_p = sb(pc, "sum_p", [P, 2], F32)
                raw = [sb(pc, f"raw{r}", [T, NH, VW], F32) for r in range(2)]
                o_sum = [sb(pc, f"o_sum{r}", [T, NH, DH], F32) for r in range(2)]
                rden = [sb(pc, f"rden_c{r}", [T, NH], F32) for r in range(2)]
                oT_hi = [sb(pc, f"oT_hi{r}", [P, NH, T], F16) for r in range(2)]
                oT_lo = [sb(pc, f"oT_lo{r}", [P, NH, T], F16) for r in range(2)]

                s_w, s_bias, s_b1, s_b2 = sem("c_w"), sem("c_bias"), sem("c_b1"), sem("c_b2")
                s_raw = [sem(f"c_raw{r}") for r in range(2)]
                (s_below, s_ab, s_tot, s_t, s_seed, s_rd, s_sum, s_on, s_tr, s_hi, s_lo, s_wp, s_add, s_bn) = [
                    sem("c_" + n) for n in ("below", "ab", "tot", "t", "seed", "rd", "sum", "on", "tr", "hi", "lo",
                                            "wp", "add", "bn")]
                with nc.Block() as block:

                    @block.sync
                    def _(sp):
                        def load_raw(b):
                            for r in range(2):
                                sp.wait_ge(s_on, b + (r + 1))
                                sp.dma_start(raw[r][:, :, :].rearrange("p h w -> p (h w)"),
                                             o_dram[bass.ds((b + r) * T, T), :]).then_inc(s_raw[r], 16)

                        load_raw(0)
                        sp.dma_start(bout_b[:, :], bout.unsqueeze(0).broadcast_to([T, D])).then_inc(s_bias, 16)
                        sp.dma_start(w32[0][:, :].rearrange("p (k n) -> p k n", k=2),
                                     W1T.rearrange("(k p) n -> p k n", p=P)).then_inc(s_w, 16)
                        sp.dma_start(w32[1][:, :].rearrange("p (k n) -> p k n", k=FF // P),
                                     W2T.rearrange("(k p) n -> p k n", p=P)).then_inc(s_w, 16)
                        sp.dma_start(b2_b[:, :], b2.unsqueeze(0).broadcast_to([T, D])).then_inc(s_b2, 16)
                        sp.dma_start(b1s[:, :], b1).then_inc(s_b1, 16)
                        with counted(sp, 2, NB, 2) as b:
                            load_raw(b)
                        sp.wait_ge(s_b2, 16)
                        sp.wait_ge(s_b1, 16)

                    @block.gpsimd
                    def _(g):

                        def add_parts(b):
                            for r in range(2):
                                g.wait_ge(s_raw[r], b * 8 + 16)
                                g.wait_ge(s_tr, b + (r + 1))
                                g.tensor_tensor(o_sum[r][:, :, :], raw[r][:, :, 0:DH], raw[r][:, :, DH + 1:VW],
                                                ALU.add).then_inc(s_sum, 1)

                        add_parts(0)
                        g.wait_ge(s_bias, 16)
                        with g.Fori(0, NB) as b:
                            g.tensor_tensor(res[:, b, :], res[:, b, :], bout_b[:, :], ALU.add).then_inc(s_seed, 1)
                        with counted(g, 2, NB, 2) as b:
                            add_parts(b)
                        g.wait_ge(s_t, 3)
                        for i in range(2):
                            g.tensor_scalar(below[i][:, :], w32[i][:, :], below_of[:, i:i + 1], 0.0,
                                            ALU.is_lt, ALU.add).then_inc(s_below, 1)

                    @block.vector
                    def _(v):
                        def weight_sums():
                            v.wait_ge(s_w, 32)
                            for i in range(2):
                                v.tensor_reduce(sum_p[:, i:i + 1], w32[i][:, :], AX.X, ALU.add,
                                                apply_absolute_value=True).then_inc(s_ab, 1)

                        def thresholds():
                            v.wait_ge(s_tot, 1)
                            v.tensor_scalar(scale[:, :], psum[:, 7, 0:2], 1.0 / (D * FF), 1e-8,
                                            ALU.mult, ALU.max).then_inc(s_t, 1)
                            v.wait_ge(s_t, 1)
                            v.tensor_scalar(above_of[:, :], scale[:, :], 0.5, None, ALU.mult).then_inc(s_t, 1)
                            v.tensor_scalar(below_of[:, :], scale[:, :], -0.5, None, ALU.mult).then_inc(s_t, 1)

                        def ternary():
                            for i in range(2):
                                v.wait_ge(s_below, i + 1)
                                wt = (w1t, w2t)[i][:, :, :].rearrange("p k n -> p (k n)")
                                v.scalar_tensor_tensor(wt, w32[i][:, :], above_of[:, i:i + 1], below[i][:, :],
                                                       ALU.is_gt, ALU.subtract).then_inc(s_ab, 1)

                        def normalise(b, r):
                            v.wait_ge(s_raw[r], b * 8 + 16)
                            v.reciprocal(rden[r][:, :], raw[r][:, :, DH]).then_inc(s_rd, 1)
                            v.wait_ge(s_rd, b + (r + 1))
                            v.wait_ge(s_sum, b + (r + 1))
                            v.tensor_tensor(o_sum[r][:, :, :], o_sum[r][:, :, :],
                                            rden[r][:, :].unsqueeze(2).broadcast_to([T, NH, DH]),
                                            ALU.mult).then_inc(s_on, 1)

                        def low(b, r):
                            v.wait_ge(s_hi, b + (r + 1))
                            v.tensor_tensor(oT_lo[r][:, :, :].rearrange("p (c h) t -> p c (h t)", c=2),
                                            psum[:, 2 * r:2 * r + 2, 0:4 * T],
                                            oT_hi[r][:, :, :].rearrange("p (c h) t -> p c (h t)", c=2),
                                            ALU.subtract).then_inc(s_lo, 1)

                        def residual(b, r):
                            v.wait_ge(s_wp, b + (r + 3))
                            v.scalar_tensor_tensor(res[:, b + r, :], psum[0:T, 4 + r, 0:D], 1 / WSCALE,
                                                   res[:, b + r, :], ALU.mult, ALU.add).then_inc(s_add, 1)
                            v.wait_ge(s_add, b + (r + 3))
                            v.bn_stats(stats[:, b + r, :], res[:, b + r, :]).then_inc(s_bn, 1)

                        credit(v, s_lo, 2)
                        credit(v, s_on, 2)
                        credit(v, s_add, 2)
                        for r in range(2):
                            normalise(0, r)
                        weight_sums()
                        thresholds()
                        v.wait_ge(s_seed, NB)
                        with counted(v, 0, NB - 2, 2) as b:
                            for r in range(2):
                                low(b, r)
                            for r in range(2):
                                normalise(b + 2, r)
                            for r in range(2):
                                residual(b, r)
                        for r in range(2):
                            low(NB - 2, r)
                        ternary()
                        for r in range(2):
                            residual(NB - 2, r)

                    @block.scalar
                    def _(a):
                        with counted(a, 0, NB, 2) as b:
                            for r in range(2):
                                a.wait_ge(s_tr, b + (r + 3))
                                a.wait_ge(s_wp, b + (r + 1))
                                a.activation(oT_hi[r][:, :, :].rearrange("p (c h) t -> p c (h t)", c=2),
                                             psum[:, 2 * r:2 * r + 2, 0:4 * T], ACT.Copy).then_inc(s_hi, 1)

                    @block.tensor
                    def _(pe):
                        def transposes(b):
                            for r in range(2):
                                pe.wait_ge(s_on, b + (r + 3))
                                pe.wait_ge(s_lo, b + (r + 1))
                                for h in range(NH):
                                    mm = pe.transpose(psum[:, 2 * r + h // 4, (h % 4) * T:(h % 4 + 1) * T],
                                                      o_sum[r][:, h, :], ident[0:T, 0:T])
                                mm.then_inc(s_tr, 1)

                        def project(b):
                            for r in range(2):
                                pe.wait_ge(s_lo, b + (r + 3))
                                pe.wait_ge(s_add, b + (r + 1))
                                for n, (h, o, w) in enumerate([(h, o, w) for h in range(NH) for o, w in (
                                        (oT_hi, wout_hi), (oT_hi, wout_lo), (oT_lo, wout_hi))]):
                                    mm = pe.matmul(psum[0:T, 4 + r, 0:D], lhsT=o[r][:, h, :], rhs=w[:, h, :],
                                                   start=(n == 0), stop=(n == 3 * NH - 1))
                                mm.then_inc(s_wp, 1)

                        credit(pe, s_tr, 2)
                        credit(pe, s_wp, 2)
                        transposes(0)
                        pe.wait_ge(s_ab, 2)
                        pe.matmul(psum[:, 7, 0:2], lhsT=ones[:, :], rhs=sum_p[:, :],
                                  start=True, stop=True).then_inc(s_tot, 1)
                        project(0)
                        with counted(pe, 2, NB, 2) as b:
                            transposes(b)
                            project(b)

            layer_norm("ln2_")

            with ExitStack() as pd:
                h32 = [sb(pd, f"h32_{r}", [P, QC], F32) for r in range(2)]
                hT_hi = sb(pd, "hT_hi", [P, FF // P, QC], F16)
                hT_lo = sb(pd, "hT_lo", [P, FF // P, QC], F16)
                (s_f1, s_ge, s_hh, s_hl, s_f2, s_seed, s_add, s_bn) = [
                    sem("d_" + n) for n in ("f1", "ge", "hh", "hl", "f2", "seed", "add", "bn")]
                NF, NI = FF // P, QC // T
                with nc.Block() as block:

                    @block.tensor
                    def _(pe):
                        credit(pe, s_f2, NI)
                        with pe.Fori(0, NQC) as c:
                            cols = bass.ds(c * QC, QC)
                            for f in range(NF):
                                pe.wait_ge(s_ge, c * NF + f + 1)
                                for n, (k, y) in enumerate([(k, y) for k in range(2) for y in (yT_hi, yT_lo)]):
                                    mm = pe.matmul(psum[:, f % 4, 0:QC], lhsT=w1t[:, k, f * P:(f + 1) * P],
                                                   rhs=y[:, k, cols], start=(n == 0), stop=(n == 3))
                                mm.then_inc(s_f1, 1)
                            pe.wait_ge(s_hl, c * NF + NF + 2)
                            for i in range(NI):
                                pe.wait_ge(s_add, c * NI + i + 1)
                                for n, (f, y) in enumerate([(f, y) for f in range(NF) for y in (hT_hi, hT_lo)]):
                                    mm = pe.matmul(psum[0:T, 4 + i, 0:D], lhsT=y[:, f, i * T:(i + 1) * T],
                                                   rhs=w2t[:, f, :], start=(n == 0), stop=(n == 2 * NF - 1))
                                mm.then_inc(s_f2, 1)

                    @block.scalar
                    def _(a):
                        credit(a, s_ge, 4)
                        with a.Fori(0, NQC) as c:
                            for f in range(NF):
                                a.wait_ge(s_f1, c * NF + f + 1)
                                a.wait_ge(s_hl, c * NF + f + 1)
                                a.activation(h32[f % 2][:, :], psum[:, f % 4, 0:QC], ACT.Gelu,
                                             bias=b1s[:, f:f + 1]).then_inc(s_ge, 1)

                    @block.vector
                    def _(v):
                        credit(v, s_hl, 2)
                        credit(v, s_add, 4)
                        v.wait_ge(s_seed, NB)
                        with v.Fori(0, NQC) as c:
                            v.wait_ge(s_f2, c * NI + NI)
                            for f in range(NF):
                                v.wait_ge(s_ge, c * NF + f + 5)
                                v.tensor_copy(hT_hi[:, f, :], h32[f % 2][:, :]).then_inc(s_hh, 1)
                                v.wait_ge(s_hh, c * NF + f + 1)
                                v.tensor_tensor(hT_lo[:, f, :], h32[f % 2][:, :], hT_hi[:, f, :],
                                                ALU.subtract).then_inc(s_hl, 1)
                            for i in range(NI):
                                v.wait_ge(s_f2, c * NI + NI + i + 1)
                                v.tensor_tensor(res[:, c * NI + i, :], psum[0:T, 4 + i, 0:D],
                                                res[:, c * NI + i, :], ALU.add).then_inc(s_add, 1)
                                v.wait_ge(s_add, c * NI + i + 5)
                                v.bn_stats(stats[:, c * NI + i, :], res[:, c * NI + i, :]).then_inc(s_bn, 1)

                    @block.gpsimd
                    def _(g):
                        with g.Fori(0, NB) as b:
                            g.tensor_tensor(res[:, b, :], res[:, b, :], b2_b[:, :], ALU.add).then_inc(s_seed, 1)

            layer_norm("ln3_", to_dram=True)


def kernel(**inputs):
    import numpy as np
    import concourse.bacc as bacc
    from concourse.bass_utils import run_bass_kernel_spmd

    i = {name: np.asarray(a) for name, a in inputs.items()}
    wq = i["L0_attn_Wq"].reshape(D, NG, NJ, DH_S).transpose(0, 2, 1, 3)
    wk = i["L0_attn_Wk"].reshape(D, NG, DH_S)
    pad = DPAD - DH_S
    wq = np.pad(wq, ((0, 0), (0, 0), (0, 0), (0, pad))).reshape(D, NJ * P)
    wk = np.pad(wk, ((0, 0), (0, 0), (0, pad))).reshape(D, P)
    laid = {
        "xT": i["x"].reshape(NT, D).T, "x": i["x"].reshape(NT, D),
        "WA": np.concatenate([wq, wk, i["L0_attn_Wv"]], axis=1), "Wo": i["L0_attn_Wo"],
        "ctxT": i["ctx_768"].reshape(NKEY, CD).T,
        "Wq": i["L0_xattn_Wq"], "Wk": i["L0_xattn_Wk"], "Wv": i["L0_xattn_Wv"],
        "Wout": i["L0_xattn_Wout"], "bout": i["L0_xattn_bout"],
        "W1T": i["L0_ffn_W1"].T, "b1": i["L0_ffn_b1"].reshape(FF // P, P).T, "W2T": i["L0_ffn_W2"].T, "b2": i["L0_ffn_b2"],
    }
    nc = bacc.Bacc("TRN2", target_bir_lowering=False, num_devices=1)
    arrays, args = {}, {}
    for name, a in laid.items():
        arrays["in_" + name] = np.ascontiguousarray(a)
        args[name] = nc.dram_tensor("in_" + name, a.shape, mybir.dt.from_np(a.dtype), kind="ExternalInput").ap()
    o_dram = nc.dram_tensor("o_scratch", (NT, NH * VW), F32, kind="Internal").ap()
    out = nc.dram_tensor("out_dram", (NT, D), F32, kind="ExternalOutput").ap()
    build(nc, **args, o_dram=o_dram, out=out)
    r = run_bass_kernel_spmd(nc, [arrays], core_ids=[0])
    return r.results[0]["out_dram"].reshape(NB, T, D)
```

```python
from contextlib import ExitStack

import concourse.bass as bass
from concourse import mybir

F32 = mybir.dt.float32
F16 = mybir.dt.float16
ALU = mybir.AluOpType
ACT = mybir.ActivationFunctionType
AX = mybir.AxisListType

P = 128
NB, T, D = 16, 112, 256
NT = NB * T
NH_S, NG, DH_S = 16, 4, 16
NJ = NH_S // NG
DPAD = 32
SC, CD = 375, 192
NKEY = NB * SC
NH, DH = 8, 128
INNER = NH * DH
FF = 4 * D
LN_EPS = 1e-5
WSCALE = 32.0

NKT = -(-NKEY // P)
LAST_KEYS = NKEY - (NKT - 1) * P
GT = 4
NGRP = -(-NKT // GT)
QB = 256
NQB = NT // QB
QT = QB // P
KC = 500
NKC = NKEY // KC
QC = 448
NQC = NT // QC
VW = 2 * DH + 1
KPAD = NKT * P - NKEY
CPAD = NGRP * GT * P - NKEY
SIM_SCALE = 1.5 * DH ** -0.5
LIFT = 5.545177444479562 / SIM_SCALE

WA_Q, WA_K, WA_V = 0, NJ * P, NJ * P + P
WA_N = WA_V + NG * DH_S

CH = 1000
W12 = D * FF // P
WP = W12 // 4


def build(nc, xT, x, WA, Wo, ctxT, Wq, Wk, Wv, Wout, bout, W1T, b1, W2T, b2, o_dram, out):
    with ExitStack() as top:
        def sb(stack, name, shape, dt):
            return stack.enter_context(nc.sbuf_tensor(name, shape, dt))

        def sem(name):
            return top.enter_context(nc.semaphore(name))

        def credit(eng, s, n):
            eng.sem_inc(s, n)

        psum = top.enter_context(nc.psum_tensor("psum", [P, 8, 512], F32))

        res = sb(top, "res", [T, NB, D], F32)
        yT_hi = sb(top, "yT_hi", [P, 2, NT], F16)
        yT_lo = sb(top, "yT_lo", [P, 2, NT], F16)
        ident = sb(top, "ident", [P, P], F32)
        ones = sb(top, "ones", [P, P], F32)
        wout_hi = sb(top, "wout_hi", [P, NH, D], F16)
        wout_lo = sb(top, "wout_lo", [P, NH, D], F16)
        stats = sb(top, "stats", [T, NB, 6], F32)
        meanvar = sb(top, "meanvar", [T, NB, 2], F32)
        rstd = sb(top, "rstd", [T, NB], F32)
        rows = [sb(top, f"rows{r}", [P, D], F32) for r in range(2)]
        norm_buf = [t[0:T, :] for t in rows]
        bout_b = sb(top, "bout_b", [T, D], F32)
        b1s = sb(top, "b1s", [P, FF // P], F32)
        context = sb(top, "context", [P, 3 * (NKEY + CPAD)], F16)
        ctx_hi, ctx_lo, ctx_s = [context[:, i * (NKEY + CPAD):(i + 1) * (NKEY + CPAD)] for i in range(3)]
        w32 = context[:, 0:4 * W12].bitcast(F32)[:, 0:2 * W12]
        w12t = context[:, 4 * W12:6 * W12]
        raw0 = context[0:T, 6 * W12:6 * W12 + 2 * NH * VW].bitcast(F32).rearrange("p (h w) -> p h w", h=NH)
        b2_b = context[0:T, 6 * W12 + 2 * NH * VW:6 * W12 + 2 * NH * VW + 2 * D].bitcast(F32)
        s_raw, s_b2 = [sem(f"raw{r}") for r in range(2)], sem("b2")

        def counted(eng, start, end, step):
            return eng.Fori(start, end - step + 1, step)

        def chain(eng, s):
            n = [0]

            def run(ins):
                n[0] += 1
                ins.then_inc(s, 1)
                eng.wait_ge(s, n[0])
            return run

        class LayerNorm:

            def __init__(self, tag, first_bank):
                self.bank = first_bank
                self.agg, self.sq, self.n, self.t, self.hi, self.lo, self.cp = [
                    sem(tag + n) for n in ("agg", "sqrt", "norm", "tr", "hi", "lo", "copy")]

            def statistics(self, v):
                for b in range(NB):
                    v.bn_aggr(meanvar[:, b, :], stats[:, b, :]).then_inc(self.agg, 1)
                v.wait_ge(self.agg, NB)
                v.tensor_scalar(rstd[:, :], meanvar[:, :, 1], LN_EPS, None, ALU.add).then_inc(self.agg, 1)
                v.wait_ge(self.sq, 1)
                v.reciprocal(rstd[:, :], rstd[:, :]).then_inc(self.agg, 1)
                v.wait_ge(self.agg, NB + 2)

            def roots(self, a):
                a.wait_ge(self.agg, NB + 1)
                a.activation(rstd[:, :], rstd[:, :], ACT.Sqrt).then_inc(self.sq, 1)

            def normalise(self, v, b, r):
                v.wait_ge(self.cp, b + 1)
                v.wait_ge(self.t, b + 1)
                v.tensor_scalar(norm_buf[r][:, :], res[:, b, :], meanvar[:, b, 0:1],
                                rstd[:, bass.ds(b, 1)], ALU.subtract, ALU.mult).then_inc(self.n, 1)

            def keep(self, g, b, r, bias):
                g.wait_ge(self.n, b + 1)
                g.tensor_tensor(res[:, b, :], norm_buf[r][:, :], bias, ALU.add).then_inc(self.cp, 1)

            def transpose(self, pe, b, r):
                pe.wait_ge(self.n, b + 1)
                pe.wait_ge(self.lo, b + 1)
                for k in range(2):
                    mm = pe.transpose(psum[:, self.bank + r, k * T:(k + 1) * T], norm_buf[r][:, k * P:(k + 1) * P],
                                      ident[0:T, 0:T])
                mm.then_inc(self.t, 1)

            def high(self, a, b, r):
                a.wait_ge(self.t, b + 3)
                a.activation(yT_hi[:, :, bass.ds(b * T, T)],
                             psum[:, self.bank + r, 0:2 * T].rearrange("p (k t) -> p k t", k=2),
                             ACT.Copy).then_inc(self.hi, 1)

            def low(self, v, b, r):
                v.wait_ge(self.hi, b + 1)
                v.tensor_tensor(yT_lo[:, :, bass.ds(b * T, T)],
                                psum[:, self.bank + r, 0:2 * T].rearrange("p (k t) -> p k t", k=2),
                                yT_hi[:, :, bass.ds(b * T, T)], ALU.subtract).then_inc(self.lo, 1)

        with ExitStack() as ab:
            wq_hi = sb(ab, "wq_hi", [P, 2, INNER], F16)
            wq_lo = sb(ab, "wq_lo", [P, 2, INNER], F16)
            wkv = {n: [sb(ab, f"w{n}_{part}", [P, INNER], F16) for part in ("hi", "lo", "s_hi", "s_lo")]
                   for n in "kv"}

            with ExitStack() as pa:
                scratch = sb(pa, "scratch", [P, 6 * 8 * T], F32)
                x32 = scratch[:, 0:2 * NT].rearrange("p (k t) -> p k t", k=2)
                wa32 = scratch[:, 2 * NT:2 * NT + 2 * WA_N].rearrange("p (k n) -> p k n", k=2)
                tiles = [scratch[0:T, i * 8 * T:(i + 1) * 8 * T].rearrange("p (h t) -> p h t", h=8)
                         for i in range(6)]
                shifted, prob, probT = tiles[0:2], tiles[2:4], tiles[4:6]
                wa_hi = sb(pa, "wa_hi", [P, 2, WA_N], F16)
                wa_lo = sb(pa, "wa_lo", [P, 2, WA_N], F16)
                wo32 = sb(pa, "wo32", [P, 2, D], F32)
                q_hi = sb(pa, "q_hi", [P, NJ, NT], F16)
                q_lo = sb(pa, "q_lo", [P, NJ, NT], F16)
                kb_hi = sb(pa, "kb_hi", [P, NG, NT], F16)
                kb_lo = sb(pa, "kb_lo", [P, NG, NT], F16)
                vs = sb(pa, "vs", [T, NB, NG, DH_S + 1], F32)
                stage = [sb(pa, f"stage{r}", [P, 2, INNER], F32) for r in range(2)]
                mx = [sb(pa, f"mx{r}", [T, 8], F32) for r in range(2)]
                rden = sb(pa, "rden", [T, 8], F32)
                att = rows[0][0:T, :]
                attT = rows[1][:, 0:2 * T].rearrange("p (k t) -> p k t", k=2)

                s_x, s_wa, s_wo, s_res = sem("a_x"), sem("a_wa"), sem("a_wo"), sem("a_res")
                s_bias, s_xh, s_xs = sem("a_bias"), sem("a_xh"), sem("a_xs")
                s_stage = [sem(f"a_stage{r}") for r in range(2)]
                s_staged = sem("a_staged")
                s_const, s_g, s_prep, s_split = sem("a_const"), sem("a_g"), sem("a_prep"), sem("a_split")
                s_pj, s_ph, s_pl = sem("a_pj"), sem("a_ph"), sem("a_pl")
                (s_s, s_mx, s_sub, s_exp, s_T, s_ptc, s_av, s_rd, s_nrm, s_at, s_atc, s_wop, s_add, s_bn) = [
                    sem("a_" + n) for n in ("s", "mx", "sub", "exp", "T", "ptc", "av", "rd", "nrm", "at",
                                            "atc", "wop", "add", "bn")]

                def halves(n, src):
                    return [(lambda st: st[:, 0, 0:n], src[0:P]), (lambda st: st[0:64, 1, 0:n], src[P:CD]),
                            (lambda st: st[64:P, 1, 0:n], src[P:CD])]

                tasks = [[(lambda st: st[:, :, 0:INNER], Wq.rearrange("(k p) n -> p k n", p=P))],
                         halves(INNER, Wk), halves(INNER, Wv),
                         [(lambda st: st[:, :, :].rearrange("p a b -> p (a b)")[:, 0:NH * D].rearrange(
                             "p (h n) -> p h n", h=NH), Wout.rearrange("(h d) n -> d h n", d=DH))]]
                tasks += [halves(CH, ctxT[:, c * CH:(c + 1) * CH]) for c in range(NKEY // CH)]

                with nc.Block() as block:

                    @block.sync
                    def _(sp):
                        sp.dma_start(x32[:, :, :], xT.rearrange("(k p) t -> p k t", p=P)).then_inc(s_x, 16)
                        sp.dma_start(wa32[:, :, :], WA.rearrange("(k p) n -> p k n", p=P)).then_inc(s_wa, 16)
                        sp.dma_start(wo32[:, :, :], Wo.rearrange("(k p) n -> p k n", p=P)).then_inc(s_wo, 16)
                        sp.dma_start(res[:, :, :], x.rearrange("(b t) d -> t b d", t=T)).then_inc(s_res, 16)
                        sp.dma_start(bout_b[:, :], bout.unsqueeze(0).broadcast_to([T, D])).then_inc(s_bias, 16)
                        sp.dma_start(b1s[:, :], b1).then_inc(s_bias, 16)
                        for i, task in enumerate(tasks):
                            if i >= 2:
                                sp.wait_ge(s_staged, i - 1)
                            for dst, src in task:
                                sp.dma_start(dst(stage[i % 2]), src).then_inc(s_stage[i % 2], 16)

                    @block.gpsimd
                    def _(g):
                        run = chain(g, s_g)
                        run(g.memset(ident[:, :], 0.0))
                        g.affine_select(out=ident[:, :], in_=ident[:, :], compare_op=ALU.not_equal, fill=1.0,
                                        base=0, pattern=[[-1, P]], channel_multiplier=1).then_inc(s_const, 1)
                        g.memset(ones[:, :], 1.0).then_inc(s_const, 1)
                        g.memset(kb_lo[:, :, :].bitcast(F32), 0.0).then_inc(s_prep, 1)
                        g.memset(vs[:, :, :, :], 1.0).then_inc(s_prep, 1)
                        for t in (ctx_hi, ctx_lo, ctx_s):
                            run(g.memset(t[:, NKEY:NKEY + CPAD], 0.0))
                        for n in "kv":
                            run(g.memset(wkv[n][3][64:P, :], 0.0))
                        loaded = [0, 0]
                        for i, task in enumerate(tasks):
                            st = stage[i % 2]
                            loaded[i % 2] += 16 * len(task)
                            g.wait_ge(s_stage[i % 2], loaded[i % 2])
                            if i < 4:
                                flat = st[:, :, :].rearrange("p a b -> p (a b)")[:, 0:NH * D] if i == 3 \
                                    else st[:, :, 0:INNER]
                                run(g.tensor_scalar(flat, flat, WSCALE, 1.0, ALU.mult, ALU.mult))
                            if i == 0:
                                run(g.tensor_copy(wq_hi[:, :, :], flat))
                                run(g.tensor_tensor(wq_lo[:, :, :], flat, wq_hi[:, :, :], ALU.subtract))
                            elif i in (1, 2):
                                hi, lo, s_hi, s_lo = wkv["kv"[i - 1]]
                                run(g.tensor_copy(hi[:, :], st[:, 0, 0:INNER]))
                                run(g.tensor_tensor(lo[:, :], st[:, 0, 0:INNER], hi[:, :], ALU.subtract))
                                run(g.tensor_copy(s_hi[:, :], st[:, 1, 0:INNER]))
                                run(g.tensor_tensor(s_lo[0:64, :], st[0:64, 1, 0:INNER], s_hi[0:64, :],
                                                    ALU.subtract))
                            elif i == 3:
                                hi, lo = [w[:, :, :].rearrange("p h n -> p (h n)") for w in (wout_hi, wout_lo)]
                                run(g.tensor_copy(hi, flat))
                                run(g.tensor_tensor(lo, flat, hi, ALU.subtract))
                            else:
                                c0 = (i - 4) * CH
                                hi, lo, s = [t[:, c0:c0 + CH] for t in (ctx_hi, ctx_lo, ctx_s)]
                                run(g.tensor_copy(hi, st[:, 0, 0:CH]))
                                run(g.tensor_tensor(lo, st[:, 0, 0:CH], hi, ALU.subtract))
                                run(g.tensor_copy(s, st[:, 1, 0:CH]))
                                s_low = ctx_s[64:P, c0:c0 + CH]
                                run(g.tensor_tensor(s_low, st[64:P, 1, 0:CH], s_low, ALU.subtract))
                            g.sem_inc(s_staged, 1)

                    @block.tensor
                    def _(pe):
                        pe.wait_ge(s_split, 2)
                        with pe.Fori(0, NQC) as c:
                            cols = bass.ds(c * QC, QC)
                            pe.wait_ge(s_xs, c + 1)
                            for j in range(NJ + 1):
                                pe.wait_ge(s_pl, c * 9 + (j + 1 if j < NJ else 8))
                                w = slice(WA_Q + j * P, WA_Q + (j + 1) * P)
                                for n, (k, wt, xt) in enumerate([(k, wt, xt) for k in range(2) for wt, xt in (
                                        (wa_hi, yT_hi), (wa_hi, yT_lo), (wa_lo, yT_hi))]):
                                    mm = pe.matmul(psum[:, j, 0:QC], lhsT=wt[:, k, w], rhs=xt[:, k, cols],
                                                   start=(n == 0), stop=(n == 5))
                                mm.then_inc(s_pj, 1)
                            pe.wait_ge(s_pl, c * 9 + 9)
                            for i in range(QC // T):
                                for n, (k, wt, xt) in enumerate([(k, wt, xt) for k in range(2) for wt, xt in (
                                        (wa_hi, yT_hi), (wa_hi, yT_lo), (wa_lo, yT_hi))]):
                                    mm = pe.matmul(psum[0:T, 5, i * 64:(i + 1) * 64],
                                                   lhsT=xt[:, k, bass.ds(c * QC + i * T, T)],
                                                   rhs=wt[:, k, WA_V:WA_N], start=(n == 0), stop=(n == 5))
                            mm.then_inc(s_pj, 1)

                        pe.wait_ge(s_pl, 9 + 9 * NQC)
                        pe.wait_ge(s_const, 2)
                        pe.wait_ge(s_wo, 16)

                        def scores(b, r):
                            u = b * 2 + r
                            pe.wait_ge(s_sub, u + 1)
                            tok = bass.ds(b * T, T)
                            for jj in range(2):
                                j = 2 * r + jj
                                for n, (q, k) in enumerate(((q_hi, kb_hi), (q_hi, kb_lo), (q_lo, kb_hi))):
                                    mm = pe.matmul(psum[0:T, j, 0:NG * T].rearrange("p (g t) -> p g t", g=NG),
                                                   lhsT=q[:, j, tok], rhs=k[:, :, tok],
                                                   start=(n == 0), stop=(n == 2))
                            mm.then_inc(s_s, 1)

                        def transposes(b, r):
                            u = b * 2 + r
                            pe.wait_ge(s_exp, u + 3)
                            pe.wait_ge(s_ptc, u + 1)
                            for hh in range(8):
                                mm = pe.transpose(psum[0:T, 4 + hh // 4, (hh % 4) * T:(hh % 4 + 1) * T],
                                                  prob[r][:, hh, :], ident[0:T, 0:T])
                            mm.then_inc(s_T, 1)

                        def weighted_v(b, r):
                            u = b * 2 + r
                            pe.wait_ge(s_ptc, u + 2)
                            pe.wait_ge(s_nrm, u + 1)
                            for hh in range(8):
                                mm = pe.matmul(psum[0:T, 6, hh * (DH_S + 1):(hh + 1) * (DH_S + 1)],
                                               lhsT=probT[r][:, hh, :], rhs=vs[:, b, hh % NG, :],
                                               start=True, stop=True)
                            mm.then_inc(s_av, 1)

                        def att_transposes(b):
                            pe.wait_ge(s_nrm, b * 2 + 3)
                            pe.wait_ge(s_add, b + 1)
                            for k in range(2):
                                mm = pe.transpose(psum[:, 7, k * T:(k + 1) * T], att[:, k * P:(k + 1) * P],
                                                  ident[0:T, 0:T])
                            mm.then_inc(s_at, 1)

                        def project(b):
                            pe.wait_ge(s_atc, b + 1)
                            for k in range(2):
                                mm = pe.matmul(psum[0:T, 7, D:2 * D], lhsT=attT[:, k, :], rhs=wo32[:, k, :],
                                               start=(k == 0), stop=(k == 1))
                            mm.then_inc(s_wop, 1)

                        def batch(b, first=False, last=False):
                            for r in range(2):
                                transposes(b, r)
                                if r == 1 and not first:
                                    att_transposes(b - 1)
                                if not last:
                                    scores(b + 1, r)
                                if r == 1:
                                    weighted_v(b, 0)
                                elif not first:
                                    weighted_v(b - 1, 1)
                                if r == 1 and not first:
                                    project(b - 1)

                        credit(pe, s_T, 2)
                        credit(pe, s_av, 2)
                        credit(pe, s_at, 1)
                        scores(0, 0)
                        scores(0, 1)
                        batch(0, first=True)
                        with pe.Fori(1, NB - 1) as b:
                            batch(b)
                        batch(NB - 1, last=True)
                        weighted_v(NB - 1, 1)
                        att_transposes(NB - 1)
                        project(NB - 1)

                    @block.scalar
                    def _(a):
                        a.wait_ge(s_wa, 16)
                        a.activation(wa_hi[:, :, :], wa32[:, :, :], ACT.Copy, scale=WSCALE).then_inc(s_split, 1)
                        with a.Fori(0, NQC) as c:
                            cols = bass.ds(c * QC, QC)
                            for j in range(NJ):
                                a.wait_ge(s_pj, c * 6 + j + 1)
                                a.activation(q_hi[:, j, cols], psum[:, j, 0:QC], ACT.Copy,
                                             scale=1 / WSCALE).then_inc(s_ph, 1)
                            a.wait_ge(s_pj, c * 6 + NJ + 1)
                            a.wait_ge(s_prep, 3)
                            for g in range(NG):
                                rows32 = slice(g * DPAD, (g + 1) * DPAD)
                                a.activation(kb_hi[rows32, g, cols], psum[rows32, NJ, 0:QC], ACT.Copy,
                                             scale=1 / WSCALE).then_inc(s_ph, 1)

                        def exps(b, r):
                            u = b * 2 + r
                            a.wait_ge(s_sub, u + 3)
                            a.wait_ge(s_T, u + 1)
                            a.activation(prob[r][:, :, :], shifted[r][:, :, :], ACT.Exp,
                                         scale=DH_S ** -0.5).then_inc(s_exp, 1)

                        def copy_probT(b, r):
                            u = b * 2 + r
                            a.wait_ge(s_T, u + 3)
                            a.wait_ge(s_av, u + 1)
                            a.activation(probT[r][:, :, :].rearrange("p (c h) t -> p c (h t)", c=2),
                                         psum[0:T, 4:6, 0:4 * T], ACT.Copy).then_inc(s_ptc, 1)

                        def copy_attT(b):
                            a.wait_ge(s_at, b + 2)
                            a.activation(attT[:, :, :], psum[:, 7, 0:2 * T].rearrange("p (k t) -> p k t", k=2),
                                         ACT.Copy).then_inc(s_atc, 1)

                        def batch(b, first=False, last=False):
                            for r in range(2):
                                copy_probT(b, r)
                                if r == 1 and not first:
                                    copy_attT(b - 1)
                                if not last:
                                    exps(b + 1, r)

                        credit(a, s_ptc, 1)
                        credit(a, s_exp, 2)
                        exps(0, 0)
                        exps(0, 1)
                        batch(0, first=True)
                        with a.Fori(1, NB - 1) as b:
                            batch(b)
                        batch(NB - 1, last=True)
                        copy_attT(NB - 1)

                    @block.vector
                    def _(v):
                        v.memset(kb_hi[:, :, :].bitcast(F32), 0.0).then_inc(s_prep, 1)

                        def split_x(c):
                            cols = slice(c * QC, (c + 1) * QC)
                            v.tensor_copy(yT_hi[:, :, cols], x32[:, :, cols]).then_inc(s_xh, 1)
                            v.wait_ge(s_xh, c + 1)
                            v.tensor_tensor(yT_lo[:, :, cols], x32[:, :, cols], yT_hi[:, :, cols],
                                            ALU.subtract).then_inc(s_xs, 1)

                        v.wait_ge(s_x, 16)
                        split_x(0)
                        v.wait_ge(s_split, 1)
                        v.scalar_tensor_tensor(wa_lo[:, :, :], wa32[:, :, :], WSCALE, wa_hi[:, :, :],
                                               ALU.mult, ALU.subtract).then_inc(s_split, 1)
                        for c in range(1, NQC):
                            split_x(c)
                        credit(v, s_pl, 9)
                        v.wait_ge(s_prep, 3)
                        with v.Fori(0, NQC) as c:
                            cols = bass.ds(c * QC, QC)
                            for j in range(NJ):
                                v.wait_ge(s_ph, c * 8 + j + 1)
                                v.scalar_tensor_tensor(q_lo[:, j, cols], psum[:, j, 0:QC], 1 / WSCALE,
                                                       q_hi[:, j, cols], ALU.mult, ALU.subtract).then_inc(s_pl, 1)
                            for g in range(NG):
                                rows32 = slice(g * DPAD, (g + 1) * DPAD)
                                v.wait_ge(s_ph, c * 8 + NJ + g + 1)
                                v.scalar_tensor_tensor(kb_lo[rows32, g, cols], psum[rows32, NJ, 0:QC], 1 / WSCALE,
                                                       kb_hi[rows32, g, cols], ALU.mult,
                                                       ALU.subtract).then_inc(s_pl, 1)
                            v.wait_ge(s_pj, c * 6 + 6)
                            v.tensor_scalar(vs[:, bass.ds(c * 4, 4), :, 0:DH_S],
                                            psum[0:T, 5, 0:256].rearrange("p (b g d) -> p b g d", b=4, g=NG),
                                            1 / WSCALE, None, ALU.mult).then_inc(s_pl, 1)

                        def shift(b, r):
                            u = b * 2 + r
                            sc = psum[0:T, 2 * r:2 * r + 2, 0:4 * T].rearrange("p c (h t) -> p c h t", h=4)
                            v.wait_ge(s_s, u + 1)
                            v.wait_ge(s_exp, u + 1)
                            v.tensor_reduce(mx[r][:, :].rearrange("p (c h) -> p c h", c=2), sc, AX.X,
                                            ALU.max).then_inc(s_mx, 1)
                            v.wait_ge(s_mx, u + 1)
                            for c in range(2):
                                ins = v.tensor_tensor(
                                    shifted[r][:, 4 * c:4 * c + 4, :],
                                    psum[0:T, 2 * r + c, 0:4 * T].rearrange("p (h t) -> p h t", h=4),
                                    mx[r][:, 4 * c:4 * c + 4].unsqueeze(2).broadcast_to([T, 4, T]), ALU.subtract)
                            ins.then_inc(s_sub, 1)

                        def normalise(b, r):
                            u = b * 2 + r
                            av = psum[0:T, 6, 0:8 * (DH_S + 1)].rearrange("p (h w) -> p h w", h=8)
                            v.wait_ge(s_av, u + 3)
                            v.reciprocal(rden[:, :], av[:, :, DH_S]).then_inc(s_rd, 1)
                            v.wait_ge(s_at, b + 1)
                            v.wait_ge(s_rd, u + 1)
                            heads = att[:, :].rearrange("p (g j d) -> p j g d", g=NG, j=NJ)
                            for jj in range(2):
                                ins = v.tensor_tensor(
                                    heads[:, 2 * r + jj, :, :], av[:, 4 * jj:4 * jj + 4, 0:DH_S],
                                    rden[:, 4 * jj:4 * jj + 4].unsqueeze(2).broadcast_to([T, 4, DH_S]), ALU.mult)
                            ins.then_inc(s_nrm, 1)

                        def residual(b):
                            v.wait_ge(s_wop, b + 1)
                            v.tensor_tensor(res[:, b, :], psum[0:T, 7, D:2 * D], res[:, b, :],
                                            ALU.add).then_inc(s_add, 1)
                            v.wait_ge(s_add, b + 2)
                            v.bn_stats(stats[:, b, :], res[:, b, :]).then_inc(s_bn, 1)

                        def batch(b, first=False, last=False):
                            for r in range(2):
                                if not last:
                                    shift(b + 1, r)
                                if r == 1:
                                    normalise(b, 0)
                                elif not first:
                                    normalise(b - 1, 1)
                            if not first:
                                residual(b - 1)

                        credit(v, s_sub, 2)
                        credit(v, s_nrm, 1)
                        credit(v, s_add, 1)
                        v.wait_ge(s_res, 16)
                        shift(0, 0)
                        shift(0, 1)
                        batch(0, first=True)
                        with v.Fori(1, NB - 1) as b:
                            batch(b)
                        batch(NB - 1, last=True)
                        normalise(NB - 1, 1)
                        residual(NB - 1)

            with ExitStack() as pb:
                k_hi = sb(pb, "k_hi", [P, 2, NKEY + KPAD], F16)
                k_lo = sb(pb, "k_lo", [P, 2, NKEY + KPAD], F16)
                v_all = sb(pb, "v_all", [P, NGRP * GT, VW], F16)
                q_hi = sb(pb, "qx_hi", [P, 2, QB], F16)
                q_lo = sb(pb, "qx_lo", [P, 2, QB], F16)
                shifted = [sb(pb, f"sx{r}", [P, GT, QB], F32) for r in range(2)]
                e32 = [sb(pb, f"e32_{r}", [P, GT, QB], F32) for r in range(2)]
                e_hi = [sb(pb, f"e_hi{r}", [P, GT, QB], F16) for r in range(2)]
                e_lo = [sb(pb, f"e_lo{r}", [P, GT, QB], F16) for r in range(2)]
                part_max = sb(pb, "part_max", [P, QT, NKC], F32)
                row_max = sb(pb, "row_max", [P, QT], F32)
                diag = sb(pb, "diag", [P, QB], F32)
                max_b = sb(pb, "max_b", [P, QB], F32)
                o_buf = sb(pb, "o_buf", [P, QT, VW], F32)

                (s_init, s_part, s_qk, s_sub, s_hi, s_lo, s_av, s_oev, s_od, s_rm, s_dg) = [
                    sem("b_" + n) for n in ("init", "part", "qk", "sub", "hi", "lo", "av", "oev",
                                            "od", "rm", "dg")]
                s_full = [sem(f"b_full{i}") for i in range(2)]
                s_free = [sem(f"b_free{i}") for i in range(2)]
                s_w, s_abs, s_t, s_tern = sem("b_w"), sem("b_abs"), sem("b_t"), sem("b_ternary")
                scale, above_of, below_of = [sb(pb, n, [P, 2], F32) for n in ("scale", "above_of", "below_of")]
                sum_p = sb(pb, "sum_p", [P, 8], F32)
                below = sb(pb, "below", [P, WP], F32)
                HG = NQB * NGRP
                LAST_QB = NQB - 1

                MID, MID_PARTS = (16, 12), 3
                ENDING, ENDING_PARTS = (17, 21), 1 + NGRP
                MID7 = (16, 10)
                HEAD = [LAST_QB * MID[i] + ENDING[i] for i in range(2)]
                HEAD_PARTS = LAST_QB * MID_PARTS + ENDING_PARTS

                class Turns:

                    def __init__(self, banks, parts):
                        self.banks, self.parts = list(banks), parts
                        self.more, self.more_parts = [0, 0], 0

                    def bank(self, i):
                        self.more[i] += 1
                        return self.banks[i] + self.more[i]

                    def part(self):
                        self.more_parts += 1
                        return self.parts + self.more_parts

                    def counts(self):
                        return self.banks, self.parts, list(self.more), self.more_parts

                    def rewind(self, counts):
                        self.banks, self.parts, self.more, self.more_parts = counts

                    def skip(self, banks, parts):
                        self.banks = [self.banks[i] + banks[i] for i in range(2)]
                        self.parts = self.parts + parts

                def block_turns(h, qb, kind):
                    mid, parts = (MID, MID_PARTS) if kind in ("k", "v") else (MID7, 1)
                    no_q = 0 if kind else 1
                    return Turns([h * HEAD[0] + qb * mid[0] - no_q, h * HEAD[1] + qb * mid[1]],
                                 h * HEAD_PARTS + qb * parts - no_q)

                def walk(eng, turns, kind, step):
                    def pieces(s):
                        if not kind:
                            return [], []
                        if isinstance(s, int) and s == 0:
                            return [("m", 0, (0, 0))], [("m", 1, (1, 0))]
                        if isinstance(s, int) and s < 4:
                            banks = (0, 1, 0) if kind == "v" and s > 1 else (1, 0, 0)
                            three = [("m", bank, (x % 2, x // 2)) for x, bank in enumerate(banks, 3 * s - 1)]
                            return three[:2], three[2:]
                        banks = (0, 1) if kind == "v" else (1, 0)
                        two = [("m", banks[0], (1, s + 1)), ("m", banks[1], (0, s + 2))]
                        return two, [("m", 0, (1, NKC - 1))] if isinstance(s, int) and s == 9 else []

                    def v(bank, tile_group):
                        return [("v", bank, tile_group)] if kind == "v" else []

                    def k(chunk):
                        return [("k", 1, chunk)] if kind == "k" else []

                    def ternary(piece):
                        return [] if kind else [("ternary", 0, piece)]

                    for s in range(4):
                        before, between = pieces(s)
                        sums = [("sum", 0, x) for x in range(3 * s, min(3 * s + 3, 8))] if not kind else []
                        scale = [("scale", 0, 0)] if not kind and s == 3 else []
                        step(s, s % 2, before, between + (v(1, s - 1) if s else []) + scale, sums)
                    trips = 2
                    per = [0, 0] if not kind else [2, 4] if kind == "v" else [2, 2]
                    per_parts = 2 if kind == "v" else 0
                    with eng.Fori(0, trips) as j:
                        before_loop = turns.counts()
                        turns.skip([j * n for n in per], j * per_parts)
                        for r in range(2):
                            s = j * 2 + (4 + r)
                            before, between = pieces(s)
                            step(s, r, before, between + v(1, s - 1), ternary(s - 4))
                        turns.rewind(before_loop)
                    turns.skip([trips * n for n in per], trips * per_parts)
                    for s in (8, 9):
                        before, between = pieces(s)
                        step(s, s % 2, before, between + v(1, s - 1), ternary(s - 4))
                    step(10, 0, [], ([("b", 0, 0)] if kind else []) + k(0) + v(1, 9), ternary(6))
                    step(11, 1, [("q", 0, 0)] if kind in ("k", "v", "m") else [], k(1) + v(1, 10),
                         v(0, 11) + ternary(7))

                def heads(eng, block_steps):
                    with eng.Fori(0, NH - 1) as h:
                        with eng.Fori(0, LAST_QB) as qb:
                            block_steps(h, qb, "k")
                        block_steps(h, LAST_QB, "v")
                    with eng.Fori(0, LAST_QB - 1) as qb:
                        block_steps(NH - 1, qb, "m")
                    block_steps(NH - 1, LAST_QB - 1, "l")
                    block_steps(NH - 1, LAST_QB, "")

                def after_next(h, qb):
                    return h + (qb + 2) // NQB, (qb + 2) % NQB * QB

                ln = LayerNorm("ln1_", 0)
                st_full, st_hi, st_free = sem("st_full"), sem("st_hi"), sem("st_free")
                TURN = 6
                TRIPS = 4
                QS = NKC + NGRP

                def start(eng, task, norm_first, norm_second):
                    with eng.Fori(0, TRIPS) as c:
                        for half, what in enumerate("kv"):
                            for r in range(2):
                                norm_first(c * 4 + (2 * half + r), r)
                            for x in range(3):
                                task(what, c * TURN + (3 * half + x), 3 * half + x, c * 3 + x)
                            for r in range(2):
                                norm_second(c * 4 + (2 * half + r), r)
                    for n in range(2):
                        task("q", QS + n, n, n)

                def start_maxima(eng, task):
                    with eng.Fori(0, TRIPS) as c:
                        for x in range(TURN):
                            task("m", c * TURN + (QS + 2 + x), (x + 2) % TURN, (x % 2, c * 3 + x // 2))
                    task("b", QS + 2 + 2 * NKC, (QS + 2 + 2 * NKC) % TURN, 0)


                with nc.Block() as block:

                    @block.tensor
                    def _(pe):
                        def tiles_of(step):
                            return NKT % GT if isinstance(step, int) and step == NGRP - 1 else GT

                        def scores(f, step, hp, np_, r):
                            pe.wait_ge(s_sub, f + 1)
                            for i in range(tiles_of(step)):
                                keys = bass.ds((step * GT + i) * P, P)
                                for n, (k, q) in enumerate(((k_hi, q_hi), (k_hi, q_lo), (k_lo, q_hi))):
                                    mm = pe.matmul(psum[:, 2 * r + i // 2, (i % 2) * QB:(i % 2 + 1) * QB],
                                                   lhsT=k[:, hp, keys], rhs=q[:, np_, :],
                                                   start=(n == 0), stop=(n == 2))
                            mm.then_inc(s_qk, 1)

                        def attend(f, step, r, first=False, last=False):
                            pe.wait_ge(s_lo, f + 3)
                            for i in range(tiles_of(step)):
                                for t in range(QT):
                                    start, stop = first and i == 0, last and i == tiles_of(step) - 1
                                    keys = slice(0, LAST_KEYS if stop else P)
                                    hi, lo = (e_hi, VW), (e_lo, DH + 1)
                                    for n, (e, w) in enumerate((lo, hi) if stop else (hi, lo)):
                                        mm = pe.matmul(psum[:, 4 + t, 0:w], lhsT=e[r][keys, i, t * P:(t + 1) * P],
                                                       rhs=v_all[keys, step * GT + i, 0:w],
                                                       start=start and n == 0, stop=stop and n == 1)
                            mm.then_inc(s_av, 1)

                        def side(turns, task, h, n, k0, q0):
                            what, i, index = task
                            pe.wait_ge(s_free[i], turns.bank(i))
                            products(what, 6 + i, index, h, n, k0, q0).then_inc(s_full[i], 1)

                        def start_task(what, number, b, index):
                            pe.wait_ge(st_free, number + 1)
                            h, n, k0, q0 = 0, 0, 0, 0
                            if what == "q":
                                n, q0 = index, index * QB
                            products(what, 2 + b, index, h, n, k0, q0).then_inc(st_full, 1)

                        def products(what, b, index, h, n, k0, q0):
                            hd = bass.ds(h * DH, DH)
                            bank = psum[:, b, :]
                            if what == "q":
                                for x, (k, w, y) in enumerate([(k, w, y) for k in range(2) for w, y in (
                                        (wq_hi, yT_hi), (wq_hi, yT_lo), (wq_lo, yT_hi))]):
                                    mm = pe.matmul(bank[:, 0:QB], lhsT=w[:, k, hd], rhs=y[:, k, bass.ds(q0, QB)],
                                                   start=(x == 0), stop=(x == 5))
                            elif what == "k":
                                whi, wlo, wshi, wslo = wkv["k"]
                                for x, (w, y) in enumerate(((whi, ctx_hi), (whi, ctx_lo), (wlo, ctx_hi),
                                                            (wshi, ctx_s), (wslo, ctx_s))):
                                    mm = pe.matmul(bank[:, 0:KC], lhsT=w[:, hd],
                                                   rhs=y[:, bass.ds((k0 + index) * KC, KC)],
                                                   start=(x == 0), stop=(x == 4))
                            elif what == "v":
                                whi, wlo, wshi, wslo = wkv["v"]
                                for g in range(GT):
                                    keys = bass.ds((index * GT + g) * P, P)
                                    for x, (y, w) in enumerate(((ctx_hi, whi), (ctx_hi, wlo), (ctx_lo, whi),
                                                                (ctx_s, wshi), (ctx_s, wslo))):
                                        mm = pe.matmul(bank[:, g * DH:(g + 1) * DH], lhsT=y[:, keys],
                                                       rhs=w[:, hd], start=(x == 0), stop=(x == 4))
                            elif what == "m":
                                t, piece = index
                                mm = pe.matmul(bank[:, 0:KC], lhsT=q_hi[:, n & 1, t * P:(t + 1) * P],
                                               rhs=k_hi[:, h & 1, bass.ds(piece * KC, KC)], start=True, stop=True)
                            elif what == "scale":
                                pe.wait_ge(s_abs, 8)
                                mm = pe.matmul(bank[:, 0:8], lhsT=ones[:, :], rhs=sum_p[:, :],
                                               start=True, stop=True)
                            else:
                                pe.wait_ge(s_dg, n + 1)
                                mm = pe.matmul(bank[:, 0:QB], lhsT=ones[:, :], rhs=diag[:, :],
                                               start=True, stop=True)
                            return mm

                        def block_steps(h, qb, kind):
                            n = h * NQB + qb
                            f0 = n * NGRP
                            turns = block_turns(h, qb, kind)
                            h1 = h + 1 if kind == "v" else h

                            def sides(tasks):
                                for task in tasks:
                                    if task[0] in ("sum", "ternary"):
                                        continue
                                    if task[0] == "q":
                                        h2, q2 = after_next(h, qb)
                                        side(turns, task, h2, n + 2, 0, q2)
                                    else:
                                        side(turns, task, h + 1 if task[0] == "k" else h1, n + 1, qb * 2, 0)

                            def step(s, r, before, between, after):
                                sides(before)
                                if isinstance(s, int) and s >= NGRP - 2:
                                    if kind:
                                        scores(f0 + s + 2, s + 2 - NGRP, h1 & 1, (n + 1) & 1, r)
                                else:
                                    scores(f0 + s + 2, s + 2, h & 1, n & 1, r)
                                sides(between)
                                first = isinstance(s, int) and s == 0
                                if first:
                                    pe.wait_ge(s_oev, n + 1)
                                attend(f0 + s, s, r, first, isinstance(s, int) and s == NGRP - 1)
                                sides(after)

                            walk(pe, turns, kind, step)

                        credit(pe, s_av, 2)
                        pe.wait_ge(s_init, 4)
                        credit(pe, ln.t, 2)
                        start(pe, start_task, lambda b, r: None, lambda b, r: ln.transpose(pe, b, r))
                        pe.wait_ge(ln.lo, NB + 2)
                        pe.wait_ge(st_hi, QS + 1)
                        start_maxima(pe, start_task)
                        pe.wait_ge(st_free, QS + 2 + 2 * NKC + TURN)
                        scores(0, 0, 0, 0, 0)
                        scores(1, 1, 0, 0, 1)
                        heads(pe, block_steps)

                    @block.scalar
                    def _(a):
                        def exp_full(f, r):
                            a.wait_ge(s_sub, f + 3)
                            a.wait_ge(s_lo, f + 1)
                            a.activation(e32[r][:, :, :], shifted[r][:, :, :], ACT.Exp,
                                         scale=SIM_SCALE)

                        def exp_hi(f, r):
                            a.wait_ge(s_av, f + 1)
                            a.activation(e_hi[r][:, :, :], shifted[r][:, :, :], ACT.Exp,
                                         scale=SIM_SCALE).then_inc(s_hi, 1)

                        def exps(f, r):
                            exp_full(f, r)
                            exp_hi(f, r)

                        def block_steps(n, groups):
                            with counted(a, 2, min(groups, NGRP), 2) as s:
                                for r in range(2):
                                    exps(n * NGRP + s + r, r)
                            if groups > NGRP:
                                exps(n * NGRP + NGRP, 0)
                                exp_full(n * NGRP + NGRP + 1, 1)
                            a.wait_ge(s_av, n * NGRP + NGRP + 2)
                            a.wait_ge(s_od, n * 16 + 16)
                            a.activation(o_buf[:, :, :], psum[:, 4:6, 0:VW], ACT.Copy).then_inc(s_oev, 1)
                            if groups > NGRP:
                                exp_hi(n * NGRP + NGRP + 1, 1)

                        def start_task(what, number, b, index):
                            a.wait_ge(st_full, number + 1)
                            if what == "q":
                                dst, src = q_hi[:, index, :], psum[:, 2 + b, 0:QB]
                            elif what == "k":
                                dst, src = k_hi[:, 0, bass.ds(index * KC, KC)], psum[:, 2 + b, 0:KC]
                            else:
                                dst = v_all[:, bass.ds(index * GT, GT), 0:DH]
                                src = psum[:, 2 + b, :].rearrange("p (g d) -> p g d", g=GT)
                            a.activation(dst, src, ACT.Copy, scale=1 / WSCALE).then_inc(st_hi, 1)

                        ln.roots(a)
                        start(a, start_task, lambda b, r: None, lambda b, r: ln.high(a, b, r))
                        credit(a, s_hi, 2)
                        credit(a, s_oev, 1)
                        exps(0, 0)
                        exps(1, 1)
                        with a.Fori(0, NH * NQB - 1) as n:
                            block_steps(n, NGRP + 2)
                        block_steps(NH * NQB - 1, NGRP)

                    @block.vector
                    def _(v):
                        def shift(f, r, sides_within=lambda: None):
                            v.wait_ge(s_qk, f + 1)
                            v.wait_ge(s_hi, f + 1)
                            for c in range(2):
                                if c == 1:
                                    sides_within()
                                ins = v.tensor_tensor(
                                    shifted[r][:, 2 * c:2 * c + 2, :],
                                    psum[:, 2 * r + c, :].rearrange("p (i q) -> p i q", i=2),
                                    max_b[:, :].unsqueeze(1).broadcast_to([P, 2, QB]), ALU.subtract)
                            ins.then_inc(s_sub, 1)

                        def split(turns, dst_hi, dst_lo, src):
                            v.tensor_scalar(dst_hi, src, 1 / WSCALE, None, ALU.mult).then_inc(s_part, 1)
                            v.wait_ge(s_part, turns.part())
                            return low_part(dst_hi, dst_lo, src)

                        def low_part(dst_hi, dst_lo, src):
                            return v.scalar_tensor_tensor(dst_lo, src, 1 / WSCALE, dst_hi, ALU.mult, ALU.subtract)

                        def parts_of(what, b, index, h, n, k0):
                            if what == "q":
                                return q_hi[:, n & 1, :], q_lo[:, n & 1, :], psum[:, b, 0:QB]
                            if what == "k":
                                cols = bass.ds((k0 + index) * KC, KC)
                                return k_hi[:, h & 1, cols], k_lo[:, h & 1, cols], psum[:, b, 0:KC]
                            tiles4 = bass.ds(index * GT, GT)
                            return (v_all[:, tiles4, 0:DH], v_all[:, tiles4, DH + 1:VW],
                                    psum[:, b, :].rearrange("p (g d) -> p g d", g=GT))

                        def piece_max(b, index):
                            t, piece = index
                            return v.tensor_reduce(part_max[:, t, bass.ds(piece, 1)], psum[:, b, 0:KC],
                                                   AX.X, ALU.max)

                        def diagonal(n):
                            v.tensor_reduce(row_max[:, :], part_max[:, :, :], AX.X, ALU.max).then_inc(s_rm, 1)
                            v.wait_ge(s_rm, n + 1)
                            v.tensor_tensor(diag[:, :].rearrange("p (t q) -> p t q", t=QT),
                                            ident[:, :].unsqueeze(1).broadcast_to([P, QT, P]),
                                            row_max[:, :].unsqueeze(2).broadcast_to([P, QT, P]),
                                            ALU.mult).then_inc(s_dg, 1)

                        def spread_maxima(b):
                            return v.tensor_scalar(max_b[:, :], psum[:, b, 0:QB], -LIFT, None, ALU.add)

                        def start_task(what, number, b, index):
                            if what in "qkv":
                                v.wait_ge(st_hi, number + 1)
                                ins = low_part(*parts_of(what, 2 + b, index, 0, index if what == "q" else 0, 0))
                            elif what == "m":
                                v.wait_ge(st_full, number + 1)
                                ins = piece_max(2 + b, index)
                            else:
                                v.wait_ge(st_free, number + TURN)
                                diagonal(0)
                                v.wait_ge(st_full, number + 1)
                                ins = spread_maxima(2 + b)
                            ins.then_inc(st_free, 1)
                            if what == "b":
                                v.wait_ge(st_free, number + TURN + 1)

                        def weights(what, piece):
                            if what == "sum":
                                v.wait_ge(s_w, 32)
                                v.tensor_reduce(sum_p[:, piece:piece + 1], w32[:, piece * WP:(piece + 1) * WP],
                                                AX.X, ALU.add, apply_absolute_value=True).then_inc(s_abs, 1)
                            else:
                                columns, of = bass.ds(piece * WP, WP), bass.ds(piece // 4, 1)
                                v.wait_ge(s_tern, piece * 2 + 1)
                                v.tensor_scalar(below[:, :], w32[:, columns], below_of[:, of], None,
                                                ALU.is_lt).then_inc(s_tern, 1)
                                v.wait_ge(s_tern, piece * 2 + 2)
                                v.scalar_tensor_tensor(w12t[:, columns], w32[:, columns], above_of[:, of],
                                                       below[:, :], ALU.is_gt, ALU.subtract).then_inc(s_tern, 1)

                        def thresholds(totals):
                            v.tensor_reduce(sum_p[:, 0:2], totals, AX.X, ALU.add).then_inc(s_t, 1)
                            v.wait_ge(s_t, 1)
                            v.tensor_scalar(scale[:, :], sum_p[:, 0:2], 1.0 / (D * FF), 1e-8,
                                            ALU.mult, ALU.max).then_inc(s_t, 1)
                            v.wait_ge(s_t, 2)
                            v.tensor_scalar(above_of[:, :], scale[:, :], 0.5, None, ALU.mult).then_inc(s_t, 1)
                            v.tensor_scalar(below_of[:, :], scale[:, :], -0.5, None, ALU.mult).then_inc(s_t, 1)
                            v.wait_ge(s_t, 4)

                        def side(turns, task, h, n, k0, q0):
                            what, i, index = task
                            if what in ("sum", "ternary"):
                                weights(what, index)
                                return
                            number = turns.bank(i)
                            if what == "scale":
                                v.wait_ge(s_full[i], number)
                                thresholds(psum[:, 6 + i, 0:8].rearrange("p (w x) -> p w x", w=2))
                                return
                            if what in "qkv":
                                v.wait_ge(s_full[i], number)
                                ins = split(turns, *parts_of(what, 6 + i, index, h, n, k0))
                            elif what == "m":
                                v.wait_ge(s_full[i], number)
                                ins = piece_max(6 + i, index)
                            else:
                                v.wait_ge(s_free[0], number)
                                v.wait_ge(s_free[1], turns.banks[1] + turns.more[1] + 1)
                                diagonal(n)
                                v.wait_ge(s_full[i], number)
                                ins = spread_maxima(6 + i)
                            ins.then_inc(s_free[i], 1)
                            if what == "b":
                                v.wait_ge(s_free[i], number + 1)

                        def block_steps(h, qb, kind):
                            n = h * NQB + qb
                            f0 = n * NGRP
                            turns = block_turns(h, qb, kind)
                            h1 = h + 1 if kind == "v" else h

                            def sides(tasks):
                                for task in tasks:
                                    side(turns, task, h + 1 if task[0] == "k" else h1,
                                         n + 2 if task[0] == "q" else n + 1, qb * 2, 0)

                            def step(s, r, before, between, after):
                                sides(before)
                                sides([t for t in between if t[0] == "b"])
                                if kind or not (isinstance(s, int) and s >= NGRP - 2):
                                    shift(f0 + s + 2, r, lambda: sides([t for t in between if t[0] == "m"][:1]))
                                sides([t for t in between if t[0] == "m"][1:])
                                sides([t for t in between if t[0] in ("k", "v", "scale")])
                                sides(after)

                            walk(v, turns, kind, step)

                        credit(v, s_sub, 2)
                        credit(v, ln.lo, 2)
                        credit(v, st_free, TURN)
                        credit(v, s_tern, 1)
                        for i in range(2):
                            credit(v, s_free[i], 1)
                        ln.statistics(v)
                        for t in (k_hi, k_lo):
                            v.memset(t[:, :, NKEY:NKEY + KPAD], 0.0).then_inc(s_init, 1)
                        v.memset(v_all[:, :, DH:DH + 1], 1.0).then_inc(s_init, 1)
                        v.memset(part_max[:, :, :], 0.0).then_inc(s_init, 1)
                        v.wait_ge(s_init, 4)
                        start(v, start_task, lambda b, r: ln.normalise(v, b, r), lambda b, r: ln.low(v, b, r))
                        start_maxima(v, start_task)
                        shift(0, 0)
                        shift(1, 1)
                        heads(v, block_steps)

                    @block.gpsimd
                    def _(g):
                        credit(g, ln.cp, 2)
                        credit(g, s_lo, 2)
                        g.wait_ge(s_bias, 32)
                        with counted(g, 0, NB, 2) as b:
                            for r in range(2):
                                ln.keep(g, b + r, r, bout_b[:, :])
                        with counted(g, 0, NH * HG, 2) as f:
                            for r in range(2):
                                g.wait_ge(s_hi, f + (r + 3))
                                g.tensor_tensor(e_lo[r][:, :, :], e32[r][:, :, :], e_hi[r][:, :, :],
                                                ALU.subtract).then_inc(s_lo, 1)

                    @block.sync
                    def _(sp):
                        credit(sp, s_od, 16)

                        def store(h, qb):
                            sp.wait_ge(s_oev, h * NQB + qb + 2)
                            sp.dma_start(o_dram[bass.ds(qb * QB, QB), bass.ds(h * VW, VW)].rearrange(
                                "(t p) w -> p t w", p=P), o_buf[:, :, :]).then_inc(s_od, 16)

                        with sp.Fori(0, NH - 1) as h:
                            with sp.Fori(0, NQB) as qb:
                                store(h, qb)
                        store(NH - 1, 0)
                        sp.dma_start(w32[:, 0:W12].rearrange("p (k n) -> p k n", k=2),
                                     W1T.rearrange("(k p) n -> p k n", p=P)).then_inc(s_w, 16)
                        sp.dma_start(w32[:, W12:2 * W12].rearrange("p (k n) -> p k n", k=FF // P),
                                     W2T.rearrange("(k p) n -> p k n", p=P)).then_inc(s_w, 16)
                        sp.dma_start(b2_b[:, :], b2.unsqueeze(0).broadcast_to([T, D])).then_inc(s_b2, 16)
                        with sp.Fori(1, LAST_QB) as qb:
                            store(NH - 1, qb)
                        sp.wait_ge(s_od, ((NH - 1) * NQB + 1) * 16 + 16)
                        sp.dma_start(raw0.rearrange("p h w -> p (h w)"), o_dram[0:T, :]).then_inc(s_raw[0], 16)
                        store(NH - 1, LAST_QB)

        with ExitStack() as cd:
            w1t = w12t[:, 0:W12].rearrange("p (k n) -> p k n", k=2)
            w2t = w12t[:, W12:2 * W12].rearrange("p (k n) -> p k n", k=FF // P)

            with ExitStack() as pc:
                raw = [raw0, sb(pc, "raw1", [T, NH, VW], F32)]
                o_sum = [sb(pc, f"o_sum{r}", [T, NH, DH], F32) for r in range(2)]
                rden = [sb(pc, f"rden_c{r}", [T, NH], F32) for r in range(2)]
                oT_hi = [sb(pc, f"oT_hi{r}", [P, NH, T], F16) for r in range(2)]
                oT_lo = [sb(pc, f"oT_lo{r}", [P, NH, T], F16) for r in range(2)]

                (s_rd, s_sum, s_on, s_tr, s_hi, s_lo, s_wp, s_add, s_bn) = [
                    sem("c_" + n) for n in ("rd", "sum", "on", "tr", "hi", "lo", "wp", "add", "bn")]
                with nc.Block() as block:

                    @block.sync
                    def _(sp):
                        def load_raw(b, r):
                            sp.wait_ge(s_rd, b + r + 1)
                            sp.wait_ge(s_sum, b + r + 1)
                            sp.dma_start(raw[r][:, :, :].rearrange("p h w -> p (h w)"),
                                         o_dram[bass.ds((b + r) * T, T), :]).then_inc(s_raw[r], 16)

                        load_raw(0, 1)
                        sp.wait_ge(s_od, NH * NQB * 16 + 16)
                        with counted(sp, 2, NB, 2) as b:
                            for r in range(2):
                                load_raw(b, r)

                    @block.gpsimd
                    def _(g):
                        credit(g, s_sum, 2)
                        with counted(g, 0, NB, 2) as b:
                            for r in range(2):
                                g.wait_ge(s_raw[r], b * 8 + 16)
                                g.wait_ge(s_tr, b + (r + 1))
                                g.tensor_tensor(o_sum[r][:, :, :], raw[r][:, :, 0:DH], raw[r][:, :, DH + 1:VW],
                                                ALU.add).then_inc(s_sum, 1)

                    @block.vector
                    def _(v):
                        def normalise(b, r):
                            v.wait_ge(s_raw[r], b * 8 + 16)
                            v.reciprocal(rden[r][:, :], raw[r][:, :, DH]).then_inc(s_rd, 1)
                            v.wait_ge(s_rd, b + (r + 3))
                            v.wait_ge(s_sum, b + (r + 3))
                            v.tensor_tensor(o_sum[r][:, :, :], o_sum[r][:, :, :],
                                            rden[r][:, :].unsqueeze(2).broadcast_to([T, NH, DH]),
                                            ALU.mult).then_inc(s_on, 1)

                        def low(b, r):
                            v.wait_ge(s_hi, b + (r + 1))
                            v.tensor_tensor(oT_lo[r][:, :, :].rearrange("p (c h) t -> p c (h t)", c=2),
                                            psum[:, 2 * r:2 * r + 2, 0:4 * T],
                                            oT_hi[r][:, :, :].rearrange("p (c h) t -> p c (h t)", c=2),
                                            ALU.subtract).then_inc(s_lo, 1)

                        def residual(b, r):
                            v.wait_ge(s_wp, b + (r + 3))
                            v.scalar_tensor_tensor(res[:, b + r, :], psum[0:T, 4 + r, 0:D], 1 / WSCALE,
                                                   res[:, b + r, :], ALU.mult, ALU.add).then_inc(s_add, 1)
                            v.wait_ge(s_add, b + (r + 3))
                            v.bn_stats(stats[:, b + r, :], res[:, b + r, :]).then_inc(s_bn, 1)

                        credit(v, s_lo, 2)
                        credit(v, s_rd, 2)
                        credit(v, s_add, 2)
                        def steps(b, normalised=True, split=True):
                            for r in range(2):
                                if normalised:
                                    normalise(b + 4, r)
                                if split:
                                    low(b + 2, r)
                                residual(b, r)

                        for r in range(2):
                            normalise(0, r)
                        for r in range(2):
                            normalise(2, r)
                            low(0, r)
                        with counted(v, 0, NB - 4, 2) as b:
                            steps(b)
                        steps(NB - 4, normalised=False)
                        steps(NB - 2, normalised=False, split=False)

                    @block.scalar
                    def _(a):
                        with counted(a, 0, NB, 2) as b:
                            for r in range(2):
                                a.wait_ge(s_tr, b + (r + 3))
                                a.wait_ge(s_wp, b + (r + 1))
                                a.activation(oT_hi[r][:, :, :].rearrange("p (c h) t -> p c (h t)", c=2),
                                             psum[:, 2 * r:2 * r + 2, 0:4 * T], ACT.Copy).then_inc(s_hi, 1)

                    @block.tensor
                    def _(pe):
                        def transposes(b, r):
                            pe.wait_ge(s_on, b + (r + 1))
                            pe.wait_ge(s_lo, b + (r + 1))
                            for h in range(NH):
                                mm = pe.transpose(psum[:, 2 * r + h // 4, (h % 4) * T:(h % 4 + 1) * T],
                                                  o_sum[r][:, h, :], ident[0:T, 0:T])
                            mm.then_inc(s_tr, 1)

                        def project(b, r):
                            pe.wait_ge(s_lo, b + (r + 3))
                            pe.wait_ge(s_add, b + (r + 1))
                            for n, (h, o, w) in enumerate([(h, o, w) for h in range(NH) for o, w in (
                                    (oT_hi, wout_hi), (oT_hi, wout_lo), (oT_lo, wout_hi))]):
                                mm = pe.matmul(psum[0:T, 4 + r, 0:D], lhsT=o[r][:, h, :], rhs=w[:, h, :],
                                               start=(n == 0), stop=(n == 3 * NH - 1))
                            mm.then_inc(s_wp, 1)

                        credit(pe, s_tr, 2)
                        credit(pe, s_wp, 2)
                        for r in range(2):
                            transposes(0, r)
                        with counted(pe, 0, NB - 2, 2) as b:
                            for r in range(2):
                                transposes(b + 2, r)
                                project(b, r)
                        for r in range(2):
                            project(NB - 2, r)

            with ExitStack() as pd:
                h32 = [sb(pd, f"h32_{r}", [P, QC], F32) for r in range(2)]
                hT_hi = sb(pd, "hT_hi", [P, FF // P, QC], F16)
                hT_lo = sb(pd, "hT_lo", [P, FF // P, QC], F16)
                NF, NI = FF // P, QC // T
                stats3, meanvar3 = sb(pd, "stats3", [T, NI, 6], F32), sb(pd, "meanvar3", [T, NI, 2], F32)
                rstd3 = sb(pd, "rstd3", [T, NI], F32)
                (s_f1, s_ge, s_hh, s_hl, s_f2, s_add, s_bn, s_agg, s_sq, s_n3, s_out) = [
                    sem("d_" + n) for n in ("f1", "ge", "hh", "hl", "f2", "add", "bn", "agg", "sq", "n3", "out")]
                ln2 = LayerNorm("ln2_", 6)
                with nc.Block() as block:

                    @block.tensor
                    def _(pe):
                        def output(c, i):
                            pe.wait_ge(s_add, c * NI + i + 1)
                            for n, (f, y) in enumerate([(f, y) for f in range(NF) for y in (hT_hi, hT_lo)]):
                                if i == 0 and y is hT_hi:
                                    pe.wait_ge(s_hl, c * NF + f + 3)
                                mm = pe.matmul(psum[0:T, 4 + i % 2, 0:D],
                                               lhsT=y[:, f, i * T:(i + 1) * T], rhs=w2t[:, f, :],
                                               start=(n == 0), stop=(n == 2 * NF - 1))
                            mm.then_inc(s_f2, 1)

                        def chunk(c, last=False):
                            pe.wait_ge(ln2.lo, c * NI + NI + 2)
                            for f in range(NF):
                                pe.wait_ge(s_ge, c * NF + f + 1)
                                for n, (k, y) in enumerate([(k, y) for k in range(2) for y in (yT_hi, yT_lo)]):
                                    mm = pe.matmul(psum[:, f % 4, 0:QC], lhsT=w1t[:, k, f * P:(f + 1) * P],
                                                   rhs=y[:, k, bass.ds(c * QC, QC)], start=(n == 0), stop=(n == 3))
                                mm.then_inc(s_f1, 1)
                            for half in range(2):
                                if not last:
                                    for r in range(2):
                                        ln2.transpose(pe, c * NI + (NI + 2 * half + r), r)
                                for r in range(2):
                                    output(c, 2 * half + r)

                        credit(pe, s_f2, NI)
                        credit(pe, ln2.t, 2)
                        for b in range(NI):
                            ln2.transpose(pe, b, b % 2)
                        with pe.Fori(0, NQC - 1) as c:
                            chunk(c)
                        chunk(NQC - 1, last=True)

                    @block.scalar
                    def _(a):
                        def chunk(c, last=False):
                            for f in range(NF):
                                a.wait_ge(s_f1, c * NF + f + 1)
                                a.wait_ge(s_hl, c * NF + f + 1)
                                ins = a.activation(h32[f % 2][:, :], psum[:, f % 4, 0:QC], ACT.Gelu,
                                                   bias=b1s[:, f:f + 1])
                                if f == 0:
                                    a.wait_ge(s_f2, c * NI + NI)
                                if f % 2 == 0:
                                    ins = a.activation(hT_hi[:, f, :], psum[:, f % 4, 0:QC], ACT.Gelu,
                                                       bias=b1s[:, f:f + 1])
                                ins.then_inc(s_ge, 1)
                            if not last:
                                for i in range(NI):
                                    ln2.high(a, c * NI + (NI + i), i % 2)
                            a.wait_ge(s_agg, c * (NI + 3) + NI + 2)
                            a.activation(rstd3[:, :], rstd3[:, :], ACT.Sqrt).then_inc(s_sq, 1)

                        credit(a, s_ge, 4)
                        ln2.roots(a)
                        a.wait_ge(s_bias, 32)
                        for b in range(NI):
                            ln2.high(a, b, b % 2)
                        with a.Fori(0, NQC - 1) as c:
                            chunk(c)
                        chunk(NQC - 1, last=True)

                    @block.vector
                    def _(v):
                        def residual(c, i):
                            b = c * NI + i
                            v.wait_ge(s_f2, b + NI + 1)
                            v.wait_ge(ln2.cp, b + 3)
                            v.tensor_tensor(res[:, b, :], psum[0:T, 4 + i % 2, 0:D], res[:, b, :],
                                            ALU.add).then_inc(s_add, 1)
                            v.wait_ge(s_add, b + 3)
                            v.sem_inc(s_bn, 1)
                            v.bn_stats(stats3[:, i, :], res[:, c * NI + i, :]).then_inc(s_bn, 1)

                        def third_norm(c):
                            v.wait_ge(s_bn, (c * NI + NI) * 2)
                            v.sem_inc(s_agg, 1)
                            for i in range(NI):
                                v.bn_aggr(meanvar3[:, i, :], stats3[:, i, :]).then_inc(s_agg, 1)
                            v.wait_ge(s_agg, c * (NI + 3) + NI + 1)
                            v.tensor_scalar(rstd3[:, :], meanvar3[:, :, 1], LN_EPS, None,
                                            ALU.add).then_inc(s_agg, 1)
                            v.wait_ge(s_sq, c + 1)
                            v.reciprocal(rstd3[:, :], rstd3[:, :]).then_inc(s_agg, 1)
                            v.wait_ge(s_agg, c * (NI + 3) + NI + 3)
                            for i in range(NI):
                                batch = res[:, c * NI + i, :]
                                v.tensor_scalar(batch, batch, meanvar3[:, i, 0:1], rstd3[:, i:i + 1],
                                                ALU.subtract, ALU.mult).then_inc(s_n3, 1)

                        def pair(step, first_batch):
                            for r in range(2):
                                step(v, first_batch + r, r)

                        def chunk(c, last=False):
                            ahead = c * NI + NI
                            if not last:
                                pair(ln2.normalise, ahead)
                            v.wait_ge(s_f2, c * NI + NI)
                            for f in range(NF):
                                v.wait_ge(s_ge, c * NF + f + 5)
                                if f % 2:
                                    v.tensor_copy(hT_hi[:, f, :], h32[f % 2][:, :]).then_inc(s_hh, 1)
                                    v.wait_ge(s_hh, c * (NF // 2) + f // 2 + 1)
                                v.tensor_tensor(hT_lo[:, f, :], h32[f % 2][:, :], hT_hi[:, f, :],
                                                ALU.subtract).then_inc(s_hl, 1)
                            if not last:
                                pair(ln2.low, ahead)
                                pair(ln2.normalise, ahead + 2)
                            for i in range(2):
                                residual(c, i)
                            if not last:
                                pair(ln2.low, ahead + 2)
                            for i in range(2):
                                residual(c, 2 + i)
                            third_norm(c)

                        credit(v, s_hl, 2)
                        credit(v, s_add, 2)
                        credit(v, ln2.lo, 2)
                        ln2.statistics(v)
                        for b in range(0, NI, 2):
                            pair(ln2.normalise, b)
                            pair(ln2.low, b)
                        with v.Fori(0, NQC - 1) as c:
                            chunk(c)
                        chunk(NQC - 1, last=True)

                    @block.gpsimd
                    def _(g):
                        credit(g, ln2.cp, 2)
                        g.wait_ge(s_b2, 16)
                        with counted(g, 0, NB, 2) as b:
                            for r in range(2):
                                ln2.keep(g, b + r, r, b2_b[:, :])

                    @block.sync
                    def _(sp):
                        with counted(sp, 0, NB, 2) as b:
                            sp.wait_ge(s_n3, b + 2)
                            sp.dma_start(out[bass.ds(b * T, 2 * T), :].rearrange("(i t) d -> t i d", t=T),
                                         res[:, bass.ds(b, 2), :]).then_inc(s_out, 16)
                        sp.wait_ge(s_out, NB * 8)


def kernel(**inputs):
    import numpy as np
    import concourse.bacc as bacc
    from concourse.bass_utils import run_bass_kernel_spmd

    i = {name: np.asarray(a) for name, a in inputs.items()}
    wq = i["L0_attn_Wq"].reshape(D, NG, NJ, DH_S).transpose(0, 2, 1, 3)
    wk = i["L0_attn_Wk"].reshape(D, NG, DH_S)
    pad = DPAD - DH_S
    wq = np.pad(wq, ((0, 0), (0, 0), (0, 0), (0, pad))).reshape(D, NJ * P)
    wk = np.pad(wk, ((0, 0), (0, 0), (0, pad))).reshape(D, P)
    laid = {
        "xT": i["x"].reshape(NT, D).T, "x": i["x"].reshape(NT, D),
        "WA": np.concatenate([wq, wk, i["L0_attn_Wv"]], axis=1), "Wo": i["L0_attn_Wo"],
        "ctxT": i["ctx_768"].reshape(NKEY, CD).T,
        "Wq": i["L0_xattn_Wq"], "Wk": i["L0_xattn_Wk"], "Wv": i["L0_xattn_Wv"],
        "Wout": i["L0_xattn_Wout"], "bout": i["L0_xattn_bout"],
        "W1T": i["L0_ffn_W1"].T, "b1": i["L0_ffn_b1"].reshape(FF // P, P).T, "W2T": i["L0_ffn_W2"].T, "b2": i["L0_ffn_b2"],
    }
    nc = bacc.Bacc("TRN2", target_bir_lowering=False, num_devices=1)
    arrays, args = {}, {}
    for name, a in laid.items():
        arrays["in_" + name] = np.ascontiguousarray(a)
        args[name] = nc.dram_tensor("in_" + name, a.shape, mybir.dt.from_np(a.dtype), kind="ExternalInput").ap()
    o_dram = nc.dram_tensor("o_scratch", (NT, NH * VW), F32, kind="Internal").ap()
    out = nc.dram_tensor("out_dram", (NT, D), F32, kind="ExternalOutput").ap()
    build(nc, **args, o_dram=o_dram, out=out)
    r = run_bass_kernel_spmd(nc, [arrays], core_ids=[0])
    return r.results[0]["out_dram"].reshape(NB, T, D)
```
